# Optimizing a Trainium2 kernel written in Bass

```python
import numpy as np
import jax
import jax.numpy as jnp

def _softmax(x, axis=-1):
    return jax.nn.softmax(x, axis=axis)

def _gelu(x):
    return jax.nn.gelu(x, approximate=True)

def _silu(x):
    return jax.nn.silu(x)

def _sigmoid(x):
    return jax.nn.sigmoid(x)

def _layernorm(x, axis=-1, eps=1e-05):
    m = jnp.mean(x, axis=axis, keepdims=True)
    v = jnp.var(x, axis=axis, keepdims=True)
    return (x - m) / jnp.sqrt(v + eps)

def _scatter_add(tgt, idx, src, axis=0):
    return tgt.at[idx].add(src)

def _segment_sum(src, seg, n):
    return jax.ops.segment_sum(src, seg, n)
kernel_name = 'mk_xattn_ffn_d1_seqx_r4_74d694'

def setup_inputs(seed: int=0):
    np.random.seed(seed)
    _w = jnp.asarray

    def _rec_inputs():
        import jax
        import jax.numpy as jnp
        _rk = jax.random.key(seed)
        x = 7.22e-05 + 1 * jax.random.normal(jax.random.fold_in(_rk, 1), (16, 256, 256), jnp.float32)
        _lenS = 256 - jax.random.randint(jax.random.fold_in(_rk, 7), (16,), 0, max(1, 256 // 4) + 1, jnp.int32)
        _lenS2 = 256 - jax.random.randint(jax.random.fold_in(_rk, 8), (16,), 0, max(1, 256 // 4) + 1, jnp.int32)
        _ctx_1024P = jax.random.normal(jax.random.fold_in(_rk, 11), (16, 16, 256), jnp.float32)
        _ctx_1024c = jax.random.dirichlet(jax.random.fold_in(_rk, 511), 0.3 * jnp.ones((16,), jnp.float32), (16, 256))
        _ctx_1024t = jnp.einsum('bsk,bkd->bsd', _ctx_1024c, _ctx_1024P)
        _ctx_1024t = _ctx_1024t * jax.lax.rsqrt(jnp.mean(jnp.square(_ctx_1024t)) + 1e-12) * 0.953939
        ctx_1024 = 4.13588e-05 + 0.999923 * (_ctx_1024t + 0.3 * jax.random.normal(jax.random.fold_in(_rk, 611), (16, 256, 256), jnp.float32))
        return (x, ctx_1024)
    x, ctx_1024 = _rec_inputs()

    def _L0_xattn_setup():
        import jax, jax.numpy as jnp
        import numpy as np
        D_MODEL = 256
        NUM_HEADS = 16
        HEAD_DIM = D_MODEL // NUM_HEADS
        B, S = (4, 512)
        key = jax.random.key(seed)
        ks = jax.random.split(key, 11)
        scale = 1.0 / np.sqrt(D_MODEL)
        return {'query': jax.random.normal(ks[0], (B, S, D_MODEL), jnp.float32), 'key': jax.random.normal(ks[1], (B, S, D_MODEL), jnp.float32), 'value': jax.random.normal(ks[2], (B, S, D_MODEL), jnp.float32), 'Wq': jax.random.normal(ks[3], (D_MODEL, D_MODEL), jnp.float32) * scale, 'bq': jnp.zeros((D_MODEL,), jnp.float32), 'Wk': jax.random.normal(ks[4], (D_MODEL, D_MODEL), jnp.float32) * scale, 'bk': jnp.zeros((D_MODEL,), jnp.float32), 'Wv': jax.random.normal(ks[5], (D_MODEL, D_MODEL), jnp.float32) * scale, 'bv': jnp.zeros((D_MODEL,), jnp.float32), 'Wo': jax.random.normal(ks[6], (D_MODEL, D_MODEL), jnp.float32) * scale, 'bo': jnp.zeros((D_MODEL,), jnp.float32)}
    _L0_xattn_all = _L0_xattn_setup()
    _L0_xattn_in = {k: v for k, v in _L0_xattn_all.items() if k in ('Wq', 'bq', 'Wk', 'bk', 'Wv', 'bv', 'Wo', 'bo')}
    del _L0_xattn_all

    def _L0_ffn_setup():
        import jax, jax.numpy as jnp
        import numpy as np
        HID = 256
        NH = 16
        NKV = 4
        HD = HID // NH
        E = 8
        TOPK = 2
        FFN = 512
        EPS = 1e-05
        THETA = 10000.0

        def _rmsnorm(x, w):
            var = jnp.mean(x * x, axis=-1, keepdims=True)
            return x * jax.lax.rsqrt(var + EPS) * w

        def _rope_tables(S):
            inv_freq = 1.0 / THETA ** (jnp.arange(0, HD, 2, dtype=jnp.float32) / HD)
            freqs = jnp.arange(S, dtype=jnp.float32)[:, None] * inv_freq[None, :]
            emb = jnp.concatenate([freqs, freqs], axis=-1)
            return (jnp.cos(emb), jnp.sin(emb))

        def _apply_rope(t, cos, sin):
            t1, t2 = jnp.split(t, 2, axis=-1)
            rot = jnp.concatenate([-t2, t1], axis=-1)
            return t * cos[None, :, None, :] + rot * sin[None, :, None, :]
        key = jax.random.key(seed)
        ks = jax.random.split(key, 6)
        B, S = (1, 512)
        x = jax.random.normal(ks[0], (B, S, HID), dtype=jnp.float32)
        wqkv = jax.random.normal(ks[1], ((NH + 2 * NKV) * HD, HID), dtype=jnp.float32) * 0.02
        wo = jax.random.normal(ks[2], (HID, NH * HD), dtype=jnp.float32) * 0.02
        gate_w = jax.random.normal(ks[3], (E, HID), dtype=jnp.float32) * 0.02
        w13 = jax.random.normal(ks[4], (E, 2 * FFN, HID), dtype=jnp.float32) * 0.02
        w2 = jax.random.normal(ks[5], (E, HID, FFN), dtype=jnp.float32) * 0.02
        return {'x': x, 'ln1_w': jnp.ones((HID,), jnp.float32), 'ln2_w': jnp.ones((HID,), jnp.float32), 'wqkv': wqkv, 'wo': wo, 'gate_w': gate_w, 'w13': w13, 'w2': w2}
    _L0_ffn_all = _L0_ffn_setup()
    _L0_ffn_in = {k: v for k, v in _L0_ffn_all.items() if k in ('ln1_w', 'ln2_w', 'wqkv', 'wo', 'gate_w', 'w13', 'w2')}
    del _L0_ffn_all
    return {'x': x, 'ctx_1024': ctx_1024, 'L0_xattn_Wq': _L0_xattn_in['Wq'], 'L0_xattn_bq': _L0_xattn_in['bq'], 'L0_xattn_Wk': _L0_xattn_in['Wk'], 'L0_xattn_bk': _L0_xattn_in['bk'], 'L0_xattn_Wv': _L0_xattn_in['Wv'], 'L0_xattn_bv': _L0_xattn_in['bv'], 'L0_xattn_Wo': _L0_xattn_in['Wo'], 'L0_xattn_bo': _L0_xattn_in['bo'], 'L0_ffn_ln1_w': _L0_ffn_in['ln1_w'], 'L0_ffn_ln2_w': _L0_ffn_in['ln2_w'], 'L0_ffn_wqkv': _L0_ffn_in['wqkv'], 'L0_ffn_wo': _L0_ffn_in['wo'], 'L0_ffn_gate_w': _L0_ffn_in['gate_w'], 'L0_ffn_w13': _L0_ffn_in['w13'], 'L0_ffn_w2': _L0_ffn_in['w2']}

def reference(x, ctx_1024, L0_xattn_Wq, L0_xattn_bq, L0_xattn_Wk, L0_xattn_bk, L0_xattn_Wv, L0_xattn_bv, L0_xattn_Wo, L0_xattn_bo, L0_ffn_ln1_w, L0_ffn_ln2_w, L0_ffn_wqkv, L0_ffn_wo, L0_ffn_gate_w, L0_ffn_w13, L0_ffn_w2):
    import jax
    import jax.numpy as jnp

    def _L0_xattn_ref(query, key, value, Wq, bq, Wk, bk, Wv, bv, Wo, bo):
        import jax, jax.numpy as jnp
        import numpy as np
        D_MODEL = 256
        NUM_HEADS = 16
        HEAD_DIM = D_MODEL // NUM_HEADS
        B, S = (4, 512)
        b = query.shape[0]

        def split_heads(x):
            return x.reshape(b, -1, NUM_HEADS, HEAD_DIM).transpose(0, 2, 1, 3)
        q = split_heads(query @ Wq.T + bq)
        k = split_heads(key @ Wk.T + bk)
        v = split_heads(value @ Wv.T + bv)
        scores = jnp.einsum('bhqd,bhkd->bhqk', q, k) / np.sqrt(HEAD_DIM)
        weights = jax.nn.softmax(scores, axis=-1)
        out = jnp.einsum('bhqk,bhkd->bhqd', weights, v)
        out = out.transpose(0, 2, 1, 3).reshape(b, -1, D_MODEL)
        return out @ Wo.T + bo

    def _L0_ffn_ref(x, ln1_w, ln2_w, wqkv, wo, gate_w, w13, w2):
        import jax, jax.numpy as jnp
        import numpy as np
        HID = 256
        NH = 16
        NKV = 4
        HD = HID // NH
        E = 8
        TOPK = 2
        FFN = 512
        EPS = 1e-05
        THETA = 10000.0

        def _rmsnorm(x, w):
            var = jnp.mean(x * x, axis=-1, keepdims=True)
            return x * jax.lax.rsqrt(var + EPS) * w

        def _rope_tables(S):
            inv_freq = 1.0 / THETA ** (jnp.arange(0, HD, 2, dtype=jnp.float32) / HD)
            freqs = jnp.arange(S, dtype=jnp.float32)[:, None] * inv_freq[None, :]
            emb = jnp.concatenate([freqs, freqs], axis=-1)
            return (jnp.cos(emb), jnp.sin(emb))

        def _apply_rope(t, cos, sin):
            t1, t2 = jnp.split(t, 2, axis=-1)
            rot = jnp.concatenate([-t2, t1], axis=-1)
            return t * cos[None, :, None, :] + rot * sin[None, :, None, :]
        B, S, _ = x.shape
        h = _rmsnorm(x, ln1_w)
        qkv = jnp.einsum('bsh,oh->bso', h, wqkv)
        q = qkv[..., :NH * HD].reshape(B, S, NH, HD)
        k = qkv[..., NH * HD:(NH + NKV) * HD].reshape(B, S, NKV, HD)
        v = qkv[..., (NH + NKV) * HD:].reshape(B, S, NKV, HD)
        cos, sin = _rope_tables(S)
        q = _apply_rope(q, cos, sin)
        k = _apply_rope(k, cos, sin)
        groups = NH // NKV
        k = jnp.repeat(k, groups, axis=2)
        v = jnp.repeat(v, groups, axis=2)
        scale = HD ** (-0.5)
        scores = jnp.einsum('bqhd,bkhd->bhqk', q, k) * scale
        causal = jnp.tril(jnp.ones((S, S), dtype=bool))
        scores = jnp.where(causal[None, None], scores, jnp.finfo(scores.dtype).min)
        probs = jax.nn.softmax(scores, axis=-1)
        attn = jnp.einsum('bhqk,bkhd->bqhd', probs, v).reshape(B, S, NH * HD)
        x = x + jnp.einsum('bso,ho->bsh', attn, wo)
        h = _rmsnorm(x, ln2_w).reshape(-1, HID)
        T = h.shape[0]
        logits = jnp.einsum('th,eh->te', h, gate_w)
        rprobs = jax.nn.softmax(logits.astype(jnp.float32), axis=-1)
        topw, topi = jax.lax.top_k(rprobs, TOPK)
        topw = topw / jnp.sum(topw, axis=-1, keepdims=True)
        wfull = jnp.zeros((T, E), jnp.float32).at[jnp.arange(T)[:, None], topi].set(topw)
        wfull = wfull.astype(h.dtype)
        out = jnp.zeros((T, HID), h.dtype)
        for e in range(E):
            w1 = w13[e, :FFN]
            w3 = w13[e, FFN:]
            g = jax.nn.silu(h @ w1.T) * (h @ w3.T)
            out = out + jnp.einsum('tf,hf->th', g, w2[e]) * wfull[:, e:e + 1]
        return x + out.reshape(B, S, HID)
    x = x + _L0_xattn_ref(_layernorm(x, axis=-1), ctx_1024, ctx_1024, L0_xattn_Wq, L0_xattn_bq, L0_xattn_Wk, L0_xattn_bk, L0_xattn_Wv, L0_xattn_bv, L0_xattn_Wo, L0_xattn_bo)
    x = x + _L0_ffn_ref(_layernorm(x, axis=-1), L0_ffn_ln1_w, L0_ffn_ln2_w, L0_ffn_wqkv, L0_ffn_wo, L0_ffn_gate_w, L0_ffn_w13, L0_ffn_w2)
    return x

_drawn_inputs = setup_inputs


def setup_inputs(seed=0):
    import zlib

    import numpy as np

    out = dict(_drawn_inputs(seed))
    spreads = {'L0_xattn_bq': (0.0, 0.392),
     'L0_xattn_bk': (0.0, 0.8),
     'L0_xattn_bv': (0.0, 0.1),
     'L0_xattn_bo': (0.0, 0.1),
     'L0_ffn_ln1_w': (1.0, 0.6),
     'L0_ffn_ln2_w': (1.0, 0.6)}
    factors = {'L0_ffn_gate_w': 7.411, 'L0_ffn_w13': 6.364, 'L0_ffn_w2': 6.35}
    for name, (base, spread) in spreads.items():
        noise = np.random.default_rng([zlib.crc32(name.encode()), seed]).standard_normal(out[name].shape)
        drawn = base * np.exp(spread * noise) if base else spread * noise
        out[name] = jnp.asarray(drawn.astype(out[name].dtype))
    for name, factor in factors.items():
        out[name] = (out[name] * factor).astype(out[name].dtype)
    return out
```

```python
from contextlib import ExitStack

import concourse.bass as bass
import numpy as np
from concourse import mybir

F32 = mybir.dt.float32
F32R = mybir.dt.float32r
I32 = mybir.dt.int32
U32 = mybir.dt.uint32
ALU = mybir.AluOpType
ACT = mybir.ActivationFunctionType
AX = mybir.AxisListType

P = 128
D = 256
DC = D // P
S = 256
TC = S // P
B = 16
PAIRS = B // 2
NH = 16
HD = D // NH
NKV = 4
HP = NH // 2
EPS = 1e-5
E = 8
FF = 512
FC = FF // P
NT = B * TC
TILES = 2 * NT + E
BANK = 512
NEG = -1.0e30
SCALE = float(HD) ** -0.5


class Sems:

    def __init__(self, nc, ctx, tag):
        self.nc, self.ctx, self.tag, self.taken = nc, ctx, tag, []

    def one(self, name):
        sem = self.ctx.enter_context(self.nc.semaphore(f"{self.tag}_{name}"))
        self.taken.append(sem.num)
        return sem

    def some(self, name, n):
        return [self.one(f"{name}{s}") for s in range(n)]

    def two(self, name):
        return self.some(name, 2)

    def clear(self):
        nums = sorted(self.taken)
        starts = [n for n in nums if n - 1 not in nums]
        ends = [n + 1 for n in nums if n + 1 not in nums]
        with self.nc.Block() as block:
            @block.gpsimd
            def _(pool):
                for start, end in zip(starts, ends):
                    pool.sem_clear(range(start, end))


def carry(eng, const):
    eng.sem_inc(const["carried"], 1)


class Banks:

    def __init__(self, const):
        self.psum, self.used = const["psum"], 0

    def take(self, shape):
        size = int(np.prod(shape[1:]))
        view = self.psum[:, self.used:self.used + size]
        self.used += -(-size // BANK) * BANK
        assert self.used <= 8 * BANK
        if len(shape) == 3:
            view = view.rearrange("p (a b) -> p a b", b=shape[2])
        return view


def project_first(nc, dram, const):
    with ExitStack() as ctx:
        def sb(name, shape, dt=F32):
            return ctx.enter_context(nc.sbuf_tensor(f"p1_{name}", shape, dt))

        sems = Sems(nc, ctx, "p1")
        wq, wk, wv = (sb(n, [P, DC, D]) for n in ("wq", "wk", "wv"))
        bq, bk = sb("bq", [P, DC]), sb("bk", [P, DC])
        bv = sb("bv", [P, D])
        x = [sb(f"x{s}", [P, TC, D]) for s in range(2)]
        c = [sb(f"c{s}", [P, TC, D]) for s in range(2)]
        st = [sb(f"st{s}", [P, TC, 6]) for s in range(2)]
        mv = [sb(f"mv{s}", [P, TC, 2]) for s in range(2)]
        ve = [sb(f"ve{s}", [P, TC]) for s in range(2)]
        rs = [sb(f"rs{s}", [P, TC]) for s in range(2)]
        xn = [sb(f"xn{s}", [P, TC, D]) for s in range(2)]
        xT = [sb(f"xT{s}", [P, DC, S]) for s in range(2)]
        cT = [sb(f"cT{s}", [P, DC, S]) for s in range(2)]
        hi = {n: [sb(f"{n}h{s}", [P, DC, S], F32R) for s in range(2)] for n in "qk"}
        lo = {n: [sb(f"{n}l{s}", [P, DC, S], F32R) for s in range(2)] for n in "qk"}
        v = [sb(f"v{s}", [P, TC, NH, HD]) for s in range(2)]
        banks = Banks(const)
        pT = {n: banks.take([P, DC, S]) for n in "xc"}
        pP = {n: [banks.take([P, 2, 256]) for s in range(2)] for n in "qkv"}

        w_in = sems.one("w_in")
        x_in, c_in = sems.two("x_in"), sems.two("c_in")
        stats, moments, eps_added, rstd = (sems.two(n) for n in ("stats", "moments", "eps_added", "rstd"))
        normed = sems.two("normed")
        turned_x, turned_c = sems.two("turned_x"), sems.two("turned_c")
        xT_out, cT_out = sems.two("xT_out"), sems.two("cT_out")
        proj = {n: sems.two(f"proj_{n}") for n in "qkv"}
        hi_out = {n: sems.two(f"hi_{n}") for n in "qk"}
        lo_out = {n: sems.two(f"lo_{n}") for n in "qk"}
        v_out = sems.two("v_out")
        qk_stored, v_stored = sems.two("qk_stored"), sems.two("v_stored")
        W_DMAS = 6 * 16

        with nc.Block() as block:
            @block.sync
            def _(sp):
                def load(i, s):
                    sp.dma_start(x[s][:], dram["x"][2 * i + s].rearrange("(t p) d -> p t d", p=P)).then_inc(x_in[s], 16)
                    sp.dma_start(c[s][:], dram["ctx"][2 * i + s].rearrange("(t p) d -> p t d", p=P)).then_inc(c_in[s], 16)

                def store(i, s):
                    b = 2 * i + s
                    for n in "qk":
                        sp.wait_ge(hi_out[n][s], DC * (i + 1))
                        sp.wait_ge(lo_out[n][s], DC * (i + 1))
                        for part, tile in (("h", hi), ("l", lo)):
                            sp.dma_start(dram[f"q1{n}{part}"][b].rearrange("(c p) t -> p c t", p=P),
                                         tile[n][s][:].bitcast(F32)).then_inc(qk_stored[s], 16)
                    sp.wait_ge(v_out[s], i + 1)
                    sp.dma_start(dram["q1v"][b].rearrange("(t p) n -> p t n", p=P),
                                 v[s][:].rearrange("p t h e -> p t (h e)")).then_inc(v_stored[s], 16)

                load(0, 0)
                for w, n in ((wq, "wq1"), (wk, "wk1"), (wv, "wv1")):
                    sp.dma_start(w[:], dram[n].rearrange("(c p) o -> p c o", p=P)).then_inc(w_in, 16)
                with nc.allow_non_contiguous_dma(reason="a column of biases"):
                    sp.dma_start(bq[:], dram["bq"].rearrange("(c p) -> p c", p=P)).then_inc(w_in, 16)
                    sp.dma_start(bk[:], dram["bk"].rearrange("(c p) -> p c", p=P)).then_inc(w_in, 16)
                sp.dma_start(bv[:], dram["bv"].partition_broadcast(P)).then_inc(w_in, 16)
                load(0, 1)
                with sp.Fori(0, PAIRS - 1) as i:
                    for s in range(2):
                        sp.wait_ge(normed[s], TC * (i + 1))
                        sp.wait_ge(turned_c[s], i + 1)
                        load(i + 1, s)
                    for s in range(2):
                        store(i, s)
                for s in range(2):
                    store(PAIRS - 1, s)
                for s in range(2):
                    sp.wait_ge(qk_stored[s], 4 * 16 * PAIRS)
                    sp.wait_ge(v_stored[s], 16 * PAIRS)

            @block.gpsimd
            def _(pool):
                with pool.Fori(0, PAIRS) as i:
                    for s in range(2):
                        pool.wait_ge(moments[s], TC * (i + 1))
                        nc.gpsimd.tensor_tensor(ve[s][:], mv[s][:, :, 1], const["eps"][:, 0:TC], ALU.add).then_inc(eps_added[s], 1)
                        pool.wait_ge(eps_added[s], i + 1)
                        nc.gpsimd.tensor_tensor(rs[s][:], ve[s][:], const["neg_half"][:, 0:TC], ALU.pow).then_inc(rstd[s], 1)

            @block.vector
            def _(dve):
                with dve.Fori(0, PAIRS) as i:
                    for s in range(2):
                        dve.wait_ge(x_in[s], 16 * (i + 1))
                        for t in range(TC):
                            nc.vector.bn_stats(st[s][:, t, :], x[s][:, t, :]).then_inc(stats[s], 1)
                        dve.wait_ge(stats[s], TC * (i + 1))
                        carry(dve, const)
                        for t in range(TC):
                            nc.vector.bn_aggr(mv[s][:, t, :], st[s][:, t, :]).then_inc(moments[s], 1)
                    for s in range(2):
                        dve.wait_ge(rstd[s], i + 1)
                        dve.wait_ge(turned_x[s], i)
                        for t in range(TC):
                            nc.vector.tensor_scalar(xn[s][:, t, :], x[s][:, t, :], mv[s][:, t, 0:1], rs[s][:, t:t + 1],
                                                    ALU.subtract, ALU.mult).then_inc(normed[s], 1)
                    for s in range(2):
                        dve.wait_ge(turned_x[s], i + 1)
                        dve.wait_ge(proj["q"][s], i)
                        nc.vector.tensor_copy(xT[s][:], pT["x"][:]).then_inc(xT_out[s], 1)
                    for s in range(2):
                        dve.wait_ge(qk_stored[s], 4 * 16 * i)
                        for n, bias in (("q", bq), ("k", bk)):
                            dve.wait_ge(hi_out[n][s], DC * (i + 1))
                            for o in range(DC):
                                nc.vector.scalar_tensor_tensor(
                                    lo[n][s][:, o, :], pP[n][s][:, o, :], bias[:, o:o + 1], hi[n][s][:, o, :].bitcast(F32),
                                    ALU.add, ALU.subtract).then_inc(lo_out[n][s], 1)
                        dve.wait_ge(proj["v"][s], i + 1)
                        dve.wait_ge(v_stored[s], 16 * i)
                        nc.vector.tensor_tensor(
                            v[s][:], pP["v"][s][:].rearrange("p t (h e) -> p t h e", h=NH),
                            bv[:].rearrange("p (u h e) -> p u h e", u=1, h=NH).to_broadcast([P, TC, NH, HD]),
                            ALU.add).then_inc(v_out[s], 1)

            @block.scalar
            def _(act):
                act.wait_ge(w_in, W_DMAS)
                with act.Fori(0, PAIRS) as i:
                    for s in range(2):
                        act.wait_ge(turned_c[s], i + 1)
                        act.wait_ge(proj["v"][s], i)
                        nc.scalar.copy(cT[s][:], pT["c"][:]).then_inc(cT_out[s], 1)
                    for s in range(2):
                        act.wait_ge(qk_stored[s], 4 * 16 * i)
                        for n, bias in (("q", bq), ("k", bk)):
                            act.wait_ge(proj[n][s], i + 1)
                            for o in range(DC):
                                nc.scalar.activation(hi[n][s][:, o, :], pP[n][s][:, o, :], ACT.Identity,
                                                     bias=bias[:, o:o + 1]).then_inc(hi_out[n][s], 1)

            @block.tensor
            def _(pe):
                pe.wait_ge(w_in, W_DMAS)
                with pe.Fori(0, PAIRS) as i:
                    for s in range(2):
                        pe.wait_ge(c_in[s], 16 * (i + 1))
                        pe.wait_ge(cT_out[1 - s], i + s)
                        for cc in range(DC):
                            for t in range(TC):
                                mm = nc.tensor.transpose(pT["c"][:, cc, t * P:(t + 1) * P], c[s][:, t, cc * P:(cc + 1) * P], const["ident"][:])
                        mm.then_inc(turned_c[s], 1)
                        pe.wait_ge(normed[s], TC * (i + 1))
                        pe.wait_ge(xT_out[1 - s], i + s)
                        for cc in range(DC):
                            for t in range(TC):
                                mm = nc.tensor.transpose(pT["x"][:, cc, t * P:(t + 1) * P], xn[s][:, t, cc * P:(cc + 1) * P], const["ident"][:])
                        mm.then_inc(turned_x[s], 1)
                    for s in range(2):
                        pe.wait_ge(cT_out[s], i + 1)
                        for n, w, src in (("k", wk, cT), ("v", None, cT), ("q", wq, xT)):
                            if n == "q":
                                pe.wait_ge(xT_out[s], i + 1)
                            if n == "v":
                                pe.wait_ge(v_out[s], i)
                                for t in range(TC):
                                    for cc in range(DC):
                                        mm = nc.tensor.matmul(pP[n][s][:, t, :], src[s][:, cc, t * P:(t + 1) * P], wv[:, cc, :],
                                                              start=(cc == 0), stop=(cc == DC - 1))
                            else:
                                pe.wait_ge(lo_out[n][s], DC * i)
                                for o in range(DC):
                                    for cc in range(DC):
                                        mm = nc.tensor.matmul(pP[n][s][:, o, :], w[:, cc, o * P:(o + 1) * P], src[s][:, cc, :],
                                                              start=(cc == 0), stop=(cc == DC - 1))
                            mm.then_inc(proj[n][s], 1)

        sems.clear()


def attention(nc, dram, const, tag, kv_heads, causal):
    SLOTS = 4
    LOOPS = B // SLOTS - 1
    GROUP = NH // kv_heads
    KG = HP if kv_heads == NH else kv_heads
    NB1 = 3 if causal else 2
    W1 = P if causal else S
    W2 = S + P if causal else 2 * S
    VW = 2 * HD
    QUADS = NH // 4
    HQ = NH // 2
    QK_DMAS = 12 * 16
    RELAY_DMAS = 4 * 16

    with ExitStack() as ctx:
        def sb(name, shape, dt=F32):
            return ctx.enter_context(nc.sbuf_tensor(f"{tag}_{name}", shape, dt))

        banks = Banks(const)

        phase_sems = Sems(nc, ctx, tag)
        sems = phase_sems.some

        qs = [sb(f"qs{u}", [P, HP, S], F32R) for u in range(SLOTS)]
        ks = [sb(f"ks{u}", [P, KG, S], F32R) for u in range(SLOTS)]
        vc = [sb(f"vc{u}", [P, TC, kv_heads, HD]) for u in range(SLOTS)]
        v = [sb(f"v{u}", [P, TC, kv_heads, VW]) for u in range(SLOTS)]
        mx = [sb(f"mx{r}", [P, NB1, P]) for r in range(2)]
        nmh = [sb(f"nmh{u}", [NH, S], F32R) for u in range(SLOTS)]
        nml = [sb(f"nml{u}", [NH, S], F32R) for u in range(SLOTS)]
        w = [sb(f"w{g}", [P, 4, W2]) for g in range(QUADS)]
        oT = [sb(f"oT{h}", [P, 2, S]) for h in range(2)]
        rec = [sb(f"rec{h}", [P, TC, HQ]) for h in range(2)]
        o = [sb(f"o{r}", [P, TC, NH, HD]) for r in range(2)]
        ps1 = [banks.take([P, 2 * S]) for r in range(2)]
        ps2 = [banks.take([P, 2, 2 * S]) for r in range(2)]
        pso = [banks.take([P, 2, S]) for h in range(2)]

        k_ones, v_ones = sems("ones", 2)
        qk_in, v_in, v_padded = sems("qk_in", SLOTS), sems("v_in", SLOTS), sems("v_padded", SLOTS)
        s1_ready, s1_used = sems("s1_ready", 2), sems("s1_used", 2)
        max_done = sems("max_done", 1)[0]
        nmh_done, relayed = sems("nmh_done", SLOTS), sems("relayed", SLOTS)
        s2_ready, exp_done = sems("s2_ready", 2), sems("exp_done", 2)
        masked, w_used = sems("masked", QUADS), sems("w_used", QUADS)
        oT_out, rec_done, o_out, o_stored = sems("oT_out", 2), sems("rec_done", 2), sems("o_out", 2), sems("o_stored", 2)

        def col(h):
            return (h % 2) * HP + h // 2

        def kslot(h):
            return h // 2 if kv_heads == NH else h // GROUP

        def items(u):
            found = []
            for p in range(HP):
                if p == 1 and u + 1 < B:
                    found.append((p, "turn", u + 1))
                if u + 2 < B:
                    found += [(p, "score", (u + 2, h)) for h in (2 * p, 2 * p + 1)]
                if p == 2 and u > 0:
                    found.append((p, "sums", (u - 1, 1)))
                if p == 6:
                    found.append((p, "sums", (u, 0)))
            return found

        FIRST = [(0, "score", (0, h)) for h in range(NH)] + [(0, "turn", 0)] + [(0, "score", (1, h)) for h in range(NH)]
        LAST = [(0, "sums", (B - 1, 1))]
        STEP = len(items(1))
        assert SLOTS * STEP % 2 == 0

        def numbered(i, u):
            n = len(FIRST) + sum(len(items(k)) for k in range(u))
            return [(p, what, x, (n + k) % 2, SLOTS * STEP // 2 * i + (n + k) // 2) for k, (p, what, x) in enumerate(items(u))]

        def first_items():
            return [(p, what, x, k % 2, k // 2) for k, (p, what, x) in enumerate(FIRST)]

        def last_items():
            n = len(FIRST) + sum(len(items(k)) for k in range(B))
            return [(0, what, x, (n + k) % 2, (n + k) // 2) for k, (_, what, x) in enumerate(LAST)]

        def steps(eng, step):
            step(0, 0)
            with eng.Fori(0, LOOPS) as i:
                for u in range(1, SLOTS + 1):
                    step(i, u)
            for u in range(SLOTS * LOOPS + 1, B):
                step(0, u)

        with nc.Block() as block:
            @block.sync
            def _(sp):
                def load(i, u):
                    b, k = SLOTS * i + u, u % SLOTS
                    for par in range(2):
                        r0 = 64 * par
                        for row, part in ((0, "h"), (HD, "l"), (2 * HD, "h")):
                            src = dram[f"{tag}q{part}"][b].rearrange("(j e r) t -> e r j t", e=2, r=HD)[par]
                            sp.dma_start(qs[k][r0 + row:r0 + row + HD, :, :].bitcast(F32), src).then_inc(qk_in[k], 16)
                        for row, part in ((0, "h"), (HD, "h"), (2 * HD, "l")):
                            if kv_heads == NH:
                                src = dram[f"{tag}k{part}"][b].rearrange("(j e r) t -> e r j t", e=2, r=HD)[par]
                            else:
                                src = dram[f"{tag}k{part}"][b].rearrange("(j r) t -> r j t", r=HD)
                            sp.dma_start(ks[k][r0 + row:r0 + row + HD, :, :].bitcast(F32), src).then_inc(qk_in[k], 16)
                    sp.dma_start(vc[k][:].rearrange("p t h e -> p t (h e)"),
                                 dram[f"{tag}v"][b].rearrange("(t p) n -> p t n", p=P)).then_inc(v_in[k], 16)

                def relay(u, q, m):
                    sp.wait_ge(s1_used[q], m + 1)
                    for par in range(2):
                        for k, part in enumerate((nmh, nml)):
                            row = 64 * par + 3 * HD + k
                            sp.dma_start(qs[u % SLOTS][row:row + 1, :, :].bitcast(F32),
                                         part[u % SLOTS][par * HP:(par + 1) * HP, :].bitcast(F32)).then_inc(relayed[u % SLOTS], 16)

                def store(i, u):
                    b = SLOTS * i + u
                    for h in range(2):
                        sp.wait_ge(o_out[h], b + 1)
                    carry(sp, const)
                    sp.dma_start(dram[f"{tag}o"][b].rearrange("(t p) d -> p t d", p=P),
                                 o[u % 2][:].rearrange("p t h e -> p t (h e)")).then_inc(o_stored[u % 2], 16)

                def relays(found):
                    for _, what, x, q, m in found:
                        if what == "turn":
                            relay(x, q, m)

                def step(i, u):
                    if u + 3 < B:
                        sp.wait_ge(w_used[QUADS - 1], SLOTS * i + u)
                        carry(sp, const)
                        load(i, u + 3)
                    relays(numbered(i, u))
                    if u > 0:
                        store(i, u - 1)

                sp.wait_ge(k_ones, 4)
                for u in range(3):
                    load(0, u)
                relays(first_items())
                steps(sp, step)
                store(0, B - 1)
                for r in range(2):
                    sp.wait_ge(o_stored[r], 16 * B // 2)

            @block.gpsimd
            def _(pool):
                for u in range(SLOTS):
                    ins = nc.gpsimd.memset(v[u][:], 1.0)
                ins.then_inc(v_ones, 1)
                pool.wait_ge(v_ones, 1)

                def pad(i, u):
                    k = u % SLOTS
                    pool.wait_ge(v_in[k], 16 * (i + u // SLOTS + 1))
                    carry(pool, const)
                    nc.gpsimd.tensor_copy(v[k][:, :, :, 0:HD], vc[k][:]).then_inc(v_padded[k], 1)

                def step(i, u):
                    if u + 2 < B:
                        pad(i, u + 2)
                    if causal:
                        for p in range(HP):
                            n = HP * u + p
                            pool.wait_ge(exp_done[n % 2], HP * SLOTS // 2 * i + n // 2 + 1)
                            carry(pool, const)
                            for e in range(2):
                                view = w[p // 2][:, 2 * (p % 2) + e, :].rearrange("p (c q) -> p c q", q=P)[:, 0:3:2, :]
                                ins = nc.gpsimd.affine_select(out=view, in_=view, compare_op=ALU.is_ge, fill=0.0, base=0,
                                                              pattern=[[0, 2], [1, P]], channel_multiplier=-1)
                            if p % 2:
                                ins.then_inc(masked[p // 2], 1)

                pad(0, 0)
                pad(0, 1)
                steps(pool, step)

            @block.vector
            def _(dve):
                def maximum(i, u, h, q, m):
                    dve.wait_ge(s1_ready[q], m + 1)
                    nc.vector.tensor_reduce(mx[u % 2][:, :, col(h)], ps1[q][:, 0:NB1 * W1].rearrange("p (c k) -> p c k", k=W1),
                                            AX.X, ALU.max).then_inc(s1_used[q], 1)
                    if causal and h == NH - 1:
                        dve.wait_ge(s1_used[1 - q], m + q)
                        dve.wait_ge(s1_used[q], m + 1)
                        nc.vector.tensor_tensor(mx[u % 2][:, 1, 0:NH], mx[u % 2][:, 1, 0:NH], mx[u % 2][:, 0, 0:NH], ALU.max).then_inc(max_done, 1)

                def negate(i, u, q, m):
                    k, g = u % SLOTS, i + u // SLOTS
                    dve.wait_ge(s1_ready[q], m + 1)
                    dve.wait_ge(relayed[k], RELAY_DMAS * g)
                    nc.vector.tensor_scalar(nmh[k][:], ps1[q][0:NH, 0:S], -1.0, None, ALU.mult).then_inc(nmh_done[k], 1)
                    dve.wait_ge(nmh_done[k], g + 1)
                    nc.vector.scalar_tensor_tensor(nml[k][:], ps1[q][0:NH, 0:S], -1.0, nmh[k][:].bitcast(F32),
                                                   ALU.mult, ALU.subtract).then_inc(s1_used[q], 1)

                def normalise(i, u, h, q, m):
                    b = SLOTS * i + u
                    sums = ps1[q][:].rearrange("p (t h e) -> p t h e", t=TC, e=VW)
                    dve.wait_ge(s1_ready[q], m + 1)
                    nc.vector.reciprocal(rec[h][:], sums[:, :, :, HD]).then_inc(rec_done[h], 1)
                    dve.wait_ge(rec_done[h], b + 1)
                    dve.wait_ge(o_stored[u % 2], 16 * ((SLOTS // 2) * i + u // 2))
                    nc.vector.tensor_tensor(o[u % 2][:, :, h * HQ:(h + 1) * HQ, :], sums[:, :, :, 0:HD],
                                            rec[h][:].rearrange("p t (h e) -> p t h e", e=1).to_broadcast([P, TC, HQ, HD]),
                                            ALU.mult).then_inc(o_out[h], 1)
                    dve.wait_ge(o_out[h], b + 1)
                    dve.sem_inc(s1_used[q], 1)

                def handle(i, found):
                    for _, what, x, q, m in found:
                        if what == "score":
                            maximum(i, *x, q, m)
                        elif what == "turn":
                            negate(i, x, q, m)
                        else:
                            normalise(i, *x, q, m)

                for u in range(SLOTS):
                    for par in range(2):
                        r0 = 64 * par + 2 * HD
                        nc.vector.memset(ks[u][r0:r0 + HD + 2, :, :].bitcast(F32), 1.0)
                for r in range(2):
                    nc.vector.memset(mx[r][:], 0.0).then_inc(k_ones, 1)
                    nc.vector.memset(ps2[r][:], 0.0).then_inc(k_ones, 1)
                dve.wait_ge(k_ones, 4)
                handle(0, first_items())
                steps(dve, lambda i, u: handle(i, numbered(i, u)))
                handle(0, last_items())

            @block.scalar
            def _(act):
                def exponentials(i, u, p):
                    n, g = HP * u + p, p // 2
                    q = n % 2
                    act.wait_ge(s2_ready[q], HP * SLOTS // 2 * i + n // 2 + 1)
                    act.wait_ge(w_used[g], SLOTS * i + u)
                    nc.scalar.activation(w[g][:, 2 * (p % 2):2 * (p % 2) + 2, :], ps2[q][:, :, 0:W2], ACT.Exp,
                                         scale=SCALE).then_inc(exp_done[q], 1)

                def sums_out(i, u, h):
                    b = SLOTS * i + u
                    act.wait_ge(w_used[2 * h + 1], b + 1)
                    act.wait_ge(o_out[h], b)
                    nc.scalar.copy(oT[h][:], pso[h][:]).then_inc(oT_out[h], 1)

                def step(i, u):
                    for p in range(HP):
                        exponentials(i, u, p)
                        if p == 0 and u > 0:
                            sums_out(i, u - 1, 1)
                        if p == 5:
                            sums_out(i, u, 0)

                steps(act, step)
                sums_out(0, B - 1, 1)

            @block.tensor
            def _(pe):
                def scores_for_max(u, h, q):
                    k = u % SLOTS
                    r0, j = 64 * (h % 2), h // 2
                    qa = qs[k][r0:r0 + 3 * HD, j, :]
                    ka = ks[k][r0:r0 + 3 * HD, kslot(h), :]
                    out = ps1[q]
                    if causal:
                        nc.tensor.matmul(out[:, 0:3 * P], const["ident_r"][:], const["mask_r"][:], start=True, stop=False)
                        nc.tensor.matmul(out[:, 0:S], qa[:, P:S], ka, start=False, stop=False)
                        return nc.tensor.matmul(out[:, S:3 * P], qa[:, 0:P], ka[:, 0:P], start=False, stop=True)
                    for t in range(TC):
                        mm = nc.tensor.matmul(out[:, t * S:(t + 1) * S], qa[:, t * P:(t + 1) * P], ka, start=True, stop=True)
                    return mm

                def scores(i, u, h):
                    n = HP * u + h // 2
                    q, k = n % 2, u % SLOTS
                    r0, j = 64 * (h % 2), h // 2
                    if h == 0:
                        pe.wait_ge(relayed[k], RELAY_DMAS * (i + u // SLOTS + 1))
                    if h % 2 == 0:
                        pe.wait_ge(exp_done[q], HP * SLOTS // 2 * i + n // 2)
                    qa = qs[k][r0:r0 + 3 * HD + 2, j, :]
                    ka = ks[k][r0:r0 + 3 * HD + 2, kslot(h), :]
                    out = ps2[q][:, h % 2, :]
                    nc.tensor.matmul(out[:, 0:S], ka[:, 0:P], qa, start=True, stop=True)
                    mm = nc.tensor.matmul(out[:, S:W2], ka[:, P:S], qa[:, P:S] if causal else qa, start=True, stop=True)
                    if h % 2 == 1:
                        mm.then_inc(s2_ready[q], 1)

                def weigh(i, u, g):
                    b, h, k = SLOTS * i + u, g // 2, u % SLOTS
                    for p in (2 * g, 2 * g + 1):
                        n = HP * u + p
                        pe.wait_ge(exp_done[n % 2], HP * SLOTS // 2 * i + n // 2 + 1)
                    if causal:
                        pe.wait_ge(masked[g], b + 1)
                    if g == 0:
                        pe.wait_ge(v_padded[k], i + u // SLOTS + 1)
                    if g % 2 == 0:
                        pe.wait_ge(oT_out[h], b)
                    for c in range(TC):
                        for e in range(4):
                            out = pso[h][32 * e:32 * e + VW, g % 2, :]
                            if causal and c:
                                out = out[:, P:S]
                            mm = nc.tensor.matmul(out, v[k][:, c, (4 * g + e) // GROUP, :],
                                                  w[g][:, e, c * S:W2 if c else S], start=(c == 0), stop=(c == TC - 1))
                    mm.then_inc(w_used[g], 1)

                def handle(i, found, p):
                    for at, what, x, q, m in found:
                        if at != p:
                            continue
                        if what == "score" and x[1] == 0:
                            pe.wait_ge(qk_in[x[0] % SLOTS], QK_DMAS * (i + x[0] // SLOTS + 1))
                        if what == "turn" and causal:
                            pe.wait_ge(max_done, SLOTS * i + x + 1)
                        if what == "turn" and not causal and x in (0, B - 1):
                            pe.wait_ge(s1_used[1 - q], m + q)
                        if what == "sums":
                            pe.wait_ge(oT_out[x[1]], SLOTS * i + x[0] + 1)
                        pe.wait_ge(s1_used[q], m)
                        if what == "score":
                            mm = scores_for_max(*x, q)
                        elif what == "turn":
                            for t in range(TC):
                                mm = nc.tensor.transpose(ps1[q][:, t * P:(t + 1) * P], mx[x % 2][:, 2 if causal and t == 0 else t, :], const["ident"][:])
                        else:
                            for t in range(TC):
                                for g in range(2):
                                    at0 = (2 * t + g) * P
                                    mm = nc.tensor.transpose(ps1[q][:, at0:at0 + P], oT[x[1]][:, g, t * P:(t + 1) * P], const["ident"][:])
                        mm.then_inc(s1_ready[q], 1)
                        yield

                def step(i, u):
                    found = numbered(i, u)
                    for p in range(HP):
                        beside = handle(i, found, p)
                        next(beside, None)
                        scores(i, u, 2 * p)
                        next(beside, None)
                        scores(i, u, 2 * p + 1)
                        for _ in beside:
                            pass
                        if p == 0 and u > 0:
                            weigh(i, u - 1, QUADS - 1)
                        if p in (2, 4, 6):
                            weigh(i, u, p // 2 - 1)

                for _ in handle(0, first_items(), 0):
                    pass
                steps(pe, step)
                weigh(0, B - 1, QUADS - 1)
                for _ in handle(0, last_items(), 0):
                    pass

        phase_sems.clear()


def middle(nc, dram, const):
    QKV = (NH + 2 * NKV) * HD
    ROPED = NH + NKV
    with ExitStack() as ctx:
        def sb(name, shape, dt=F32):
            return ctx.enter_context(nc.sbuf_tensor(f"p3_{name}", shape, dt))

        banks = Banks(const)

        sems = Sems(nc, ctx, "p3")
        wo = sb("wo", [P, DC, D])
        wqkv = sb("wqkv", [P, DC, QKV])
        bo = sb("bo", [P, D])
        ln1 = sb("ln1", [P, D])
        cos, sin = sb("cos", [P, TC, HD]), sb("sin", [P, TC, HD])
        a = [sb(f"a{s}", [P, TC, D]) for s in range(2)]
        x = [sb(f"x{s}", [P, TC, D]) for s in range(2)]
        xb = [sb(f"xb{s}", [P, TC, D]) for s in range(2)]
        aT = [sb(f"aT{s}", [P, DC, S]) for s in range(2)]
        x1 = [sb(f"x1{s}", [P, TC, D]) for s in range(2)]
        st = [sb(f"st{s}", [P, TC, 6]) for s in range(2)]
        mv = [sb(f"mv{s}", [P, TC, 2]) for s in range(2)]
        sc = [sb(f"sc{s}", [P, 6, TC]) for s in range(2)]
        z = [sb(f"z{s}", [P, TC, D]) for s in range(2)]
        h = [sb(f"h{s}", [P, TC, D]) for s in range(2)]
        hT = [sb(f"hT{s}", [P, DC, S]) for s in range(2)]
        qc = [sb(f"qc{s}", [P, TC, ROPED, HD]) for s in range(2)]
        qr = [sb(f"qr{s}", [P, TC, ROPED, HD]) for s in range(2)]
        qkv = [sb(f"qkv{s}", [P, TC, QKV]) for s in range(2)]
        qh, ql = ([sb(f"{n}{s}", [P, DC, S], F32R) for s in range(2)] for n in ("qh", "ql"))
        kh, kl = ([sb(f"{n}{s}", [NKV * HD, S], F32R) for s in range(2)] for n in ("kh", "kl"))
        pa, po, ph = banks.take([P, DC, S]), banks.take([P, TC, D]), banks.take([P, DC, S])
        pp = [banks.take([P, 2 * S])[:, 0:QKV] for t in range(TC)]
        pq, pk = banks.take([P, DC, S]), banks.take([P, 2 * S])[:, 0:S]

        w_in = sems.one("w_in")
        (a_in, x_in, biased, a_turned, aT_out, wo_done, x1_out, stats, moments, scaled, z_out, h_out, h_turned, hT_out,
         qkv_done, v_out, roped_c, roped, qk_turned, qh_out, kh_out, ql_out, kl_out, stored, x1z_stored) = (
            sems.two(n) for n in ("a_in", "x_in", "biased", "a_turned", "aT_out", "wo_done", "x1_out", "stats", "moments",
                                  "scaled", "z_out", "h_out", "h_turned", "hT_out", "qkv_done", "v_out", "roped_c", "roped",
                                  "qk_turned", "qh_out", "kh_out", "ql_out", "kl_out", "stored", "x1z_stored"))
        W_DMAS = 6 * 16

        with nc.Block() as block:
            @block.sync
            def _(sp):
                def load(i, s):
                    b = 2 * i + s
                    sp.dma_start(a[s][:], dram["q1o"][b].rearrange("(t p) d -> p t d", p=P)).then_inc(a_in[s], 16)
                    sp.dma_start(x[s][:], dram["x"][b].rearrange("(t p) d -> p t d", p=P)).then_inc(x_in[s], 16)

                def store(i, s):
                    b = 2 * i + s
                    for n, tile, ready in (("x1", x1, x1_out), ("z", z, z_out)):
                        sp.wait_ge(ready[s], i + 1)
                        carry(sp, const)
                        sp.dma_start(dram[n][b].rearrange("(t p) d -> p t d", p=P), tile[s][:]).then_inc(x1z_stored[s], 16)
                    for n, tile, ready in (("q2qh", qh, qh_out), ("q2ql", ql, ql_out)):
                        sp.wait_ge(ready[s], i + 1)
                        sp.dma_start(dram[n][b].rearrange("(c p) t -> p c t", p=P), tile[s][:].bitcast(F32)).then_inc(stored[s], 16)
                    for n, tile, ready in (("q2kh", kh, kh_out), ("q2kl", kl, kl_out)):
                        sp.wait_ge(ready[s], i + 1)
                        carry(sp, const)
                        sp.dma_start(dram[n][b], tile[s][:].bitcast(F32)).then_inc(stored[s], 16)
                    sp.dma_start(dram["q2v"][b].rearrange("(t p) n -> p t n", p=P),
                                 qkv[s][:, :, ROPED * HD:QKV]).then_inc(stored[s], 16)

                load(0, 0)
                for tile, n in ((wo, "wo1"), (wqkv, "wqkv")):
                    sp.dma_start(tile[:], dram[n].rearrange("(c p) o -> p c o", p=P)).then_inc(w_in, 16)
                for tile, n in ((cos, "cos"), (sin, "sin")):
                    sp.dma_start(tile[:], dram[n].rearrange("(t p) e -> p t e", p=P)).then_inc(w_in, 16)
                for tile, n in ((bo, "bo"), (ln1, "ln1")):
                    sp.dma_start(tile[:], dram[n].partition_broadcast(P)).then_inc(w_in, 16)
                load(0, 1)
                with sp.Fori(0, PAIRS - 1) as i:
                    for s in range(2):
                        sp.wait_ge(a_turned[s], i + 1)
                        sp.wait_ge(biased[s], i + 1)
                        carry(sp, const)
                        load(i + 1, s)
                    for s in range(2):
                        store(i, s)
                for s in range(2):
                    store(PAIRS - 1, s)
                for s in range(2):
                    sp.wait_ge(x1z_stored[s], 2 * 16 * PAIRS)
                    sp.wait_ge(stored[s], 5 * 16 * PAIRS)

            @block.gpsimd
            def _(pool):
                pool.wait_ge(w_in, W_DMAS)
                with pool.Fori(0, PAIRS) as i:
                    for s in range(2):
                        pool.wait_ge(x_in[s], 16 * (i + 1))
                        pool.wait_ge(x1_out[s], i)
                        nc.gpsimd.tensor_tensor(xb[s][:], x[s][:], bo[:].rearrange("p (t d) -> p t d", t=1).to_broadcast([P, TC, D]),
                                                ALU.add).then_inc(biased[s], 1)
                    for s in range(2):
                        var = mv[s][:, :, 1]
                        eps, half = const["eps"][:, 0:TC], const["neg_half"][:, 0:TC]
                        pool.wait_ge(moments[s], TC * (i + 1))
                        chain = [(sc[s][:, 0, :], var, eps, ALU.add), (sc[s][:, 1, :], sc[s][:, 0, :], half, ALU.pow),
                                 (sc[s][:, 2, :], var, sc[s][:, 1, :], ALU.mult), (sc[s][:, 3, :], sc[s][:, 2, :], sc[s][:, 1, :], ALU.mult),
                                 (sc[s][:, 4, :], sc[s][:, 3, :], eps, ALU.add), (sc[s][:, 5, :], sc[s][:, 4, :], half, ALU.pow)]
                        for k, (out, in0, in1, op) in enumerate(chain):
                            if k:
                                pool.wait_ge(scaled[s], len(chain) * i + k)
                            nc.gpsimd.tensor_tensor(out, in0, in1, op).then_inc(scaled[s], 1)
                    for s in range(2):
                        pool.wait_ge(roped_c[s], 3 * TC * (i + 1))
                        pool.wait_ge(stored[s], 5 * 16 * i)
                        nc.gpsimd.tensor_tensor(qkv[s][:, :, 0:ROPED * HD].rearrange("p t (h e) -> p t h e", e=HD), qc[s][:], qr[s][:],
                                                ALU.add).then_inc(roped[s], 1)

            @block.vector
            def _(dve):
                dve.wait_ge(w_in, W_DMAS)
                with dve.Fori(0, PAIRS) as i:
                    for s in range(2):
                        dve.wait_ge(wo_done[s], i + 1)
                        dve.wait_ge(biased[s], i + 1)
                        dve.wait_ge(x1z_stored[s], 2 * 16 * i)
                        nc.vector.tensor_tensor(x1[s][:], po[:], xb[s][:], ALU.add).then_inc(x1_out[s], 1)
                        dve.wait_ge(x1_out[s], i + 1)
                        for t in range(TC):
                            nc.vector.bn_stats(st[s][:, t, :], x1[s][:, t, :]).then_inc(stats[s], 1)
                        dve.wait_ge(stats[s], TC * (i + 1))
                        carry(dve, const)
                        for t in range(TC):
                            nc.vector.bn_aggr(mv[s][:, t, :], st[s][:, t, :]).then_inc(moments[s], 1)
                    for s in range(2):
                        dve.wait_ge(scaled[s], 6 * (i + 1))
                        for t in range(TC):
                            ins = nc.vector.tensor_scalar(z[s][:, t, :], x1[s][:, t, :], mv[s][:, t, 0:1], sc[s][:, 1, t:t + 1],
                                                          ALU.subtract, ALU.mult)
                        ins.then_inc(z_out[s], 1)
                        dve.wait_ge(z_out[s], i + 1)
                        dve.wait_ge(h_turned[s], i)
                        for t in range(TC):
                            ins = nc.vector.scalar_tensor_tensor(h[s][:, t, :], z[s][:, t, :], sc[s][:, 5, t:t + 1], ln1[:],
                                                                 ALU.mult, ALU.mult)
                        ins.then_inc(h_out[s], 1)
                    for s in range(2):
                        dve.wait_ge(qkv_done[s], i + 1)
                        dve.wait_ge(roped[s], i)
                        for t in range(TC):
                            heads = pp[t][:, 0:ROPED * HD].rearrange("p (h e) -> p h e", e=HD)

                            def table(tile, e0, e1):
                                return tile[:, t:t + 1, e0:e1].to_broadcast([P, ROPED, e1 - e0])

                            nc.vector.tensor_tensor(qc[s][:, t, :, :], heads, table(cos, 0, HD), ALU.mult).then_inc(roped_c[s], 1)
                            H2 = HD // 2
                            nc.vector.tensor_tensor(qr[s][:, t, :, 0:H2], heads[:, :, H2:HD], table(sin, 0, H2), ALU.mult).then_inc(roped_c[s], 1)
                            nc.vector.tensor_tensor(qr[s][:, t, :, H2:HD], heads[:, :, 0:H2], table(sin, H2, HD), ALU.mult).then_inc(roped_c[s], 1)
                    for s in range(2):
                        dve.wait_ge(qh_out[s], i + 1)
                        dve.wait_ge(stored[s], 5 * 16 * i)
                        nc.vector.tensor_tensor(ql[s][:], pq[:], qh[s][:].bitcast(F32), ALU.subtract).then_inc(ql_out[s], 1)
                        dve.wait_ge(kh_out[s], i + 1)
                        nc.vector.tensor_tensor(kl[s][:], pk[0:NKV * HD, :], kh[s][:].bitcast(F32), ALU.subtract).then_inc(kl_out[s], 1)

            @block.scalar
            def _(act):
                with act.Fori(0, PAIRS) as i:
                    for s in range(2):
                        act.wait_ge(a_turned[s], i + 1)
                        act.wait_ge(wo_done[s], i)
                        nc.scalar.copy(aT[s][:], pa[:]).then_inc(aT_out[s], 1)
                    for s in range(2):
                        act.wait_ge(h_turned[s], i + 1)
                        act.wait_ge(qkv_done[s], i)
                        nc.scalar.copy(hT[s][:], ph[:]).then_inc(hT_out[s], 1)
                    for s in range(2):
                        act.wait_ge(qkv_done[s], i + 1)
                        act.wait_ge(roped_c[s], 3 * TC * (i + 1))
                        act.wait_ge(stored[s], 5 * 16 * i)
                        for t in range(TC):
                            nc.scalar.copy(qkv[s][:, t, ROPED * HD:QKV], pp[t][:, ROPED * HD:QKV]).then_inc(v_out[s], 1)
                    for s in range(2):
                        act.wait_ge(qk_turned[s], i + 1)
                        act.wait_ge(stored[s], 5 * 16 * i)
                        nc.scalar.copy(qh[s][:], pq[:]).then_inc(qh_out[s], 1)
                        nc.scalar.copy(kh[s][:], pk[0:NKV * HD, :]).then_inc(kh_out[s], 1)

            @block.tensor
            def _(pe):
                pe.wait_ge(w_in, W_DMAS)

                def turn(out, src):
                    for c in range(DC):
                        for t in range(TC):
                            mm = nc.tensor.transpose(out[:, c, t * P:(t + 1) * P], src[:, t, c * P:(c + 1) * P], const["ident"][:])
                    return mm

                with pe.Fori(0, PAIRS) as i:
                    for s in range(2):
                        pe.wait_ge(a_in[s], 16 * (i + 1))
                        pe.wait_ge(aT_out[1 - s], i + s)
                        turn(pa, a[s]).then_inc(a_turned[s], 1)
                    for s in range(2):
                        pe.wait_ge(aT_out[s], i + 1)
                        pe.wait_ge(x1_out[1 - s], i + s)
                        for t in range(TC):
                            for c in range(DC):
                                mm = nc.tensor.matmul(po[:, t, :], aT[s][:, c, t * P:(t + 1) * P], wo[:, c, :],
                                                      start=(c == 0), stop=(c == DC - 1))
                        mm.then_inc(wo_done[s], 1)
                    for s in range(2):
                        pe.wait_ge(h_out[s], i + 1)
                        pe.wait_ge(hT_out[1 - s], i + s)
                        turn(ph, h[s]).then_inc(h_turned[s], 1)
                    for s in range(2):
                        pe.wait_ge(hT_out[s], i + 1)
                        pe.wait_ge(v_out[1 - s], TC * (i + s))
                        for t in range(TC):
                            for c in range(DC):
                                mm = nc.tensor.matmul(pp[t][:], hT[s][:, c, t * P:(t + 1) * P], wqkv[:, c, :],
                                                      start=(c == 0), stop=(c == DC - 1))
                        mm.then_inc(qkv_done[s], 1)
                    for s in range(2):
                        pe.wait_ge(roped[s], i + 1)
                        pe.wait_ge(v_out[s], TC * (i + 1))
                        pe.wait_ge(ql_out[1 - s], i + s)
                        pe.wait_ge(kl_out[1 - s], i + s)
                        for t in range(TC):
                            for c in range(DC + 1):
                                out = pq[:, c, t * P:(t + 1) * P] if c < DC else pk[:, t * P:(t + 1) * P]
                                mm = nc.tensor.transpose(out, qkv[s][:, t, c * P:(c + 1) * P], const["ident"][:])
                        mm.then_inc(qk_turned[s], 1)

        sems.clear()


def finish_attention(nc, dram, const):
    with ExitStack() as ctx:
        def sb(name, shape, dt=F32):
            return ctx.enter_context(nc.sbuf_tensor(f"p5_{name}", shape, dt))

        banks = Banks(const)

        sems = Sems(nc, ctx, "p5")
        wo = sb("wo", [P, DC, D])
        gate = sb("gate", [P, DC, E])
        ln2 = sb("ln2", [P, D])
        a = [sb(f"a{s}", [P, TC, D]) for s in range(2)]
        x1 = [sb(f"x1{s}", [P, TC, D]) for s in range(2)]
        z = [sb(f"z{s}", [P, TC, D]) for s in range(2)]
        aT = [sb(f"aT{s}", [P, DC, S]) for s in range(2)]
        z2 = [sb(f"z2{s}", [P, TC, D]) for s in range(2)]
        r = [sb(f"r{s}", [P, TC, D]) for s in range(2)]
        sq = [sb(f"sq{s}", [P, TC, D]) for s in range(2)]
        ms = [sb(f"ms{s}", [P, TC]) for s in range(2)]
        sc = [sb(f"sc{s}", [P, 3, TC]) for s in range(2)]
        h = [sb(f"h{s}", [P, TC, D]) for s in range(2)]
        hT = [sb(f"hT{s}", [P, DC, S]) for s in range(2)]
        pa = [banks.take([P, DC, S]) for s in range(2)]
        po = [banks.take([P, TC, D]) for s in range(2)]
        ph = [banks.take([P, DC, S]) for s in range(2)]
        pl = [banks.take([P, TC, E]) for s in range(2)]

        w_in = sems.one("w_in")
        (a_in, xz_in, a_turned, aT_out, wo_done, z2_out, r_out, squared, scaled, h_out, h_turned, hT_out, logits_done,
         logits_out, r_stored, h_stored) = (
            sems.two(n) for n in ("a_in", "xz_in", "a_turned", "aT_out", "wo_done", "z2_out", "r_out", "squared", "scaled",
                                  "h_out", "h_turned", "hT_out", "logits_done", "logits_out", "r_stored", "h_stored"))
        W_DMAS = 3 * 16

        with nc.Block() as block:
            @block.sync
            def _(sp):
                def load(i, s):
                    b = 2 * i + s
                    sp.dma_start(a[s][:], dram["q2o"][b].rearrange("(t p) d -> p t d", p=P)).then_inc(a_in[s], 16)
                    sp.dma_start(z[s][:], dram["z"][b].rearrange("(t p) d -> p t d", p=P)).then_inc(xz_in[s], 16)
                    sp.dma_start(x1[s][:], dram["x1"][b].rearrange("(t p) d -> p t d", p=P)).then_inc(xz_in[s], 16)

                def store(i, s):
                    b = 2 * i + s
                    for n, tile, ready, done in (("r", r, r_out, r_stored), ("h2", h, h_out, h_stored)):
                        sp.wait_ge(ready[s], i + 1)
                        carry(sp, const)
                        sp.dma_start(dram[n][b].rearrange("(t p) d -> p t d", p=P), tile[s][:]).then_inc(done[s], 16)

                load(0, 0)
                sp.dma_start(wo[:], dram["wo2"].rearrange("(c p) o -> p c o", p=P)).then_inc(w_in, 16)
                sp.dma_start(gate[:], dram["gate"].rearrange("(c p) e -> p c e", p=P)).then_inc(w_in, 16)
                sp.dma_start(ln2[:], dram["ln2"].partition_broadcast(P)).then_inc(w_in, 16)
                load(0, 1)
                with sp.Fori(0, PAIRS - 1) as i:
                    for s in range(2):
                        sp.wait_ge(a_turned[s], i + 1)
                        sp.wait_ge(r_out[s], i + 1)
                        carry(sp, const)
                        load(i + 1, s)
                    for s in range(2):
                        store(i, s)
                for s in range(2):
                    store(PAIRS - 1, s)
                for s in range(2):
                    sp.wait_ge(r_stored[s], 16 * PAIRS)
                    sp.wait_ge(h_stored[s], 16 * PAIRS)

            @block.gpsimd
            def _(pool):
                with pool.Fori(0, PAIRS) as i:
                    for s in range(2):
                        pool.wait_ge(xz_in[s], 2 * 16 * (i + 1))
                        pool.wait_ge(z2_out[s], i + 1)
                        pool.wait_ge(r_stored[s], 16 * i)
                        nc.gpsimd.tensor_tensor(r[s][:], x1[s][:], z2[s][:], ALU.add).then_inc(r_out[s], 1)
                    for s in range(2):
                        pool.wait_ge(squared[s], TC * (i + 1))
                        chain = [(sc[s][:, 0, :], ms[s][:], const["inv_d"][:, 0:TC], ALU.mult),
                                 (sc[s][:, 1, :], sc[s][:, 0, :], const["eps"][:, 0:TC], ALU.add),
                                 (sc[s][:, 2, :], sc[s][:, 1, :], const["neg_half"][:, 0:TC], ALU.pow)]
                        for k, (out, in0, in1, op) in enumerate(chain):
                            if k:
                                pool.wait_ge(scaled[s], len(chain) * i + k)
                            nc.gpsimd.tensor_tensor(out, in0, in1, op).then_inc(scaled[s], 1)

            @block.vector
            def _(dve):
                dve.wait_ge(w_in, W_DMAS)
                with dve.Fori(0, PAIRS) as i:
                    for s in range(2):
                        dve.wait_ge(wo_done[s], i + 1)
                        dve.wait_ge(xz_in[s], 2 * 16 * (i + 1))
                        dve.wait_ge(r_out[s], i)
                        nc.vector.tensor_tensor(z2[s][:], po[s][:], z[s][:], ALU.add).then_inc(z2_out[s], 1)
                    for s in range(2):
                        dve.wait_ge(scaled[s], 3 * (i + 1))
                        dve.wait_ge(h_stored[s], 16 * i)
                        for t in range(TC):
                            ins = nc.vector.scalar_tensor_tensor(h[s][:, t, :], z2[s][:, t, :], sc[s][:, 2, t:t + 1], ln2[:],
                                                                 ALU.mult, ALU.mult)
                        ins.then_inc(h_out[s], 1)
                    for s in range(2):
                        dve.wait_ge(logits_done[s], i + 1)
                        nc.vector.tensor_copy(const["logits"][:, bass.ds(2 * TC * i + TC * s, TC), :], pl[s][:]).then_inc(logits_out[s], 1)

            @block.scalar
            def _(act):
                with act.Fori(0, PAIRS) as i:
                    for s in range(2):
                        act.wait_ge(a_turned[s], i + 1)
                        act.wait_ge(wo_done[s], i)
                        nc.scalar.copy(aT[s][:], pa[s][:]).then_inc(aT_out[s], 1)
                    for s in range(2):
                        act.wait_ge(z2_out[s], i + 1)
                        act.wait_ge(scaled[s], 3 * i)
                        for t in range(TC):
                            nc.scalar.activation(sq[s][:, t, :], z2[s][:, t, :], ACT.Square, accum_out=ms[s][:, t:t + 1]).then_inc(squared[s], 1)
                    for s in range(2):
                        act.wait_ge(h_turned[s], i + 1)
                        act.wait_ge(logits_done[s], i)
                        nc.scalar.copy(hT[s][:], ph[s][:]).then_inc(hT_out[s], 1)

            @block.tensor
            def _(pe):
                pe.wait_ge(w_in, W_DMAS)

                def turn(out, src):
                    for c in range(DC):
                        for t in range(TC):
                            mm = nc.tensor.transpose(out[:, c, t * P:(t + 1) * P], src[:, t, c * P:(c + 1) * P], const["ident"][:])
                    return mm

                with pe.Fori(0, PAIRS) as i:
                    for s in range(2):
                        pe.wait_ge(a_in[s], 16 * (i + 1))
                        pe.wait_ge(aT_out[s], i)
                        turn(pa[s], a[s]).then_inc(a_turned[s], 1)
                    for s in range(2):
                        pe.wait_ge(aT_out[s], i + 1)
                        pe.wait_ge(z2_out[s], i)
                        for t in range(TC):
                            for c in range(DC):
                                mm = nc.tensor.matmul(po[s][:, t, :], aT[s][:, c, t * P:(t + 1) * P], wo[:, c, :],
                                                      start=(c == 0), stop=(c == DC - 1))
                        mm.then_inc(wo_done[s], 1)
                    for s in range(2):
                        pe.wait_ge(h_out[s], i + 1)
                        pe.wait_ge(hT_out[s], i)
                        turn(ph[s], h[s]).then_inc(h_turned[s], 1)
                    for s in range(2):
                        pe.wait_ge(hT_out[s], i + 1)
                        pe.wait_ge(logits_out[s], i)
                        for t in range(TC):
                            for c in range(DC):
                                mm = nc.tensor.matmul(pl[s][:, t, :], hT[s][:, c, t * P:(t + 1) * P], gate[:, c, :],
                                                      start=(c == 0), stop=(c == DC - 1))
                        mm.then_inc(logits_done[s], 1)

        sems.clear()


def route(nc, dram, const):
    with ExitStack() as ctx:
        def sb(name, shape, dt=F32):
            return ctx.enter_context(nc.sbuf_tensor(f"p6_{name}", shape, dt))

        big = [P, NT, E]
        lm, eq, idx, tmp, m1, m2, m, cnt, tot, incl, pos = (sb(n, big) for n in ("lm", "eq", "idx", "tmp", "m1", "m2", "m", "cnt", "tot",
                                                                                 "incl", "pos"))
        top, first, diff, ex, den = (sb(n, [P, NT]) for n in ("top", "first", "diff", "ex", "den"))
        top2 = sb("top2", [P, NT])
        ones_t = sb("ones_t", [P, NT])
        nti = sb("nti", [P, E], I32)
        ntf, cum, base = (sb(n, [P, E]) for n in ("ntf", "cum", "base"))
        le = sb("le", [P, TILES, E])
        ef = sb("ef", [P, TILES])
        banks = Banks(const)
        pc, pt = banks.take(big), banks.take(big)
        sems = Sems(nc, ctx, "p6")
        done = sems.one("done")
        counted = sems.one("counted")
        masks = sems.one("masks")
        exped = sems.one("exped")
        diffed = sems.one("diffed")

        def over_experts(tile):
            return tile[:].rearrange("p (t e) -> p t e", e=1).to_broadcast(big)

        def over_tiles(tile, n=NT):
            return tile[:].rearrange("p (t e) -> p t e", t=1).to_broadcast([P, n, E])

        with nc.Block() as block:
            @block.vector
            def _(dve):
                chain = [0]

                def link(ins):
                    chain[0] += 1
                    ins.then_inc(done, 1)
                    dve.wait_ge(done, chain[0])

                tt, v = nc.vector.tensor_tensor, nc.vector
                logits = const["logits"]

                def pick(values, best, mask):
                    link(v.tensor_reduce(best[:], values[:], AX.X, ALU.max))
                    link(tt(eq[:], values[:], over_experts(best), ALU.is_equal))
                    link(tt(idx[:], eq[:], over_tiles(const["iota_less"]), ALU.mult))
                    link(v.tensor_scalar(idx[:], idx[:], float(E), None, ALU.add))
                    link(v.tensor_reduce(first[:], idx[:], AX.X, ALU.min))
                    link(tt(mask[:], over_tiles(const["iota_e"]), over_experts(first), ALU.is_equal))

                link(v.memset(ones_t[:], 1.0))
                pick(logits, top, m1)
                link(v.tensor_scalar(tmp[:], m1[:], -3.0e38, None, ALU.mult))
                link(v.tensor_scalar(lm[:], m1[:], -1.0, 1.0, ALU.mult, ALU.add))
                link(tt(lm[:], lm[:], logits[:], ALU.mult))
                link(tt(lm[:], lm[:], tmp[:], ALU.add))
                pick(lm, top2, m2)
                link(tt(m[:], m1[:], m2[:], ALU.add))
                dve.sem_inc(masks, 1)
                link(tt(diff[:], top2[:], top[:], ALU.subtract))
                dve.sem_inc(diffed, 1)
                dve.wait_ge(counted, 1)
                link(v.tensor_copy(tot[:], pt[:]))
                for e in range(E):
                    link(v.tensor_tensor_scan(incl[:, :, e], ones_t[:], tot[:, :, e], 0.0, ALU.mult, ALU.add))
                link(v.tensor_scalar(nti[:], incl[:, NT - 1, :], float(P - 1), None, ALU.add))
                link(v.tensor_scalar(nti[:], nti[:], P.bit_length() - 1, None, ALU.arith_shift_right))
                link(v.tensor_copy(ntf[:], nti[:]))
                link(v.tensor_tensor_scan(cum[:], ones_t[:, 0:E], ntf[:], 0.0, ALU.mult, ALU.add))
                link(tt(base[:], cum[:], ntf[:], ALU.subtract))
                link(v.tensor_scalar(base[:], base[:], float(P), None, ALU.mult))
                link(tt(pos[:], incl[:], tot[:], ALU.subtract))
                link(tt(pos[:], pos[:], over_tiles(base), ALU.add))
                link(tt(pos[:], pos[:], pc[:], ALU.add))
                for k, mask in enumerate((m1, m2)):
                    link(tt(tmp[:], pos[:], mask[:], ALU.mult))
                    link(v.tensor_reduce(first[:], tmp[:], AX.X, ALU.add))
                    link(v.tensor_copy(const["rows"][:, k, :], first[:]))
                link(tt(le[:], over_tiles(cum, TILES), const["iota_j"][:].rearrange("p (t e) -> p t e", e=1).to_broadcast([P, TILES, E]),
                        ALU.is_le))
                link(v.tensor_reduce(ef[:], le[:], AX.X, ALU.add))
                link(v.tensor_scalar(ef[:], ef[:], float(E - 1), None, ALU.min))
                link(v.tensor_copy(const["expert"][:], ef[0:1, :]))
                dve.wait_ge(exped, 1)
                link(v.tensor_scalar(den[:], ex[:], 1.0, None, ALU.add))
                link(v.reciprocal(const["weight"][:, 0, :], den[:]))
                link(tt(const["weight"][:, 1, :], ex[:], const["weight"][:, 0, :], ALU.mult))

            @block.scalar
            def _(act):
                act.wait_ge(diffed, 1)
                nc.scalar.activation(ex[:], diff[:], ACT.Exp).then_inc(exped, 1)

            @block.tensor
            def _(pe):
                pe.wait_ge(masks, 1)
                flat = m[:].rearrange("p t e -> p (t e)")
                nc.tensor.matmul(pc[:].rearrange("p t e -> p (t e)"), const["before"][:], flat, start=True, stop=True)
                nc.tensor.matmul(pt[:].rearrange("p t e -> p (t e)"), const["ones"][:], flat, start=True, stop=True).then_inc(counted, 1)

        sems.clear()


def dispatch(nc, dram, const):
    RING = 4
    with ExitStack() as ctx:
        h = [ctx.enter_context(nc.sbuf_tensor(f"p7_h{k}", [P, D], F32)) for k in range(RING)]
        sems = Sems(nc, ctx, "p7")
        h_in, sent = (sems.some(n, RING) for n in ("h_in", "sent"))
        h2 = dram["h2"].rearrange("b (t p) d -> (b t) p d", p=P)
        with nc.Block() as block:
            @block.sync
            def _(sp):
                for t in range(NT):
                    if t >= RING:
                        sp.wait_ge(sent[t % RING], 32 * (t // RING))
                    sp.dma_start(h[t % RING][:], h2[t]).then_inc(h_in[t % RING], 16)

            @block.gpsimd
            def _(pool):
                for t in range(NT):
                    pool.wait_ge(h_in[t % RING], 16 * (t // RING + 1))
                    for k in range(2):
                        nc.gpsimd.indirect_dma_start(
                            dram["xs"], bass.IndirectOffsetOnAxis(ap=const["rows"][:, k, t:t + 1], axis=0), h[t % RING][:], None,
                            bounds_check=TILES * P - 1).then_inc(sent[t % RING], 16)
                for k in range(RING):
                    pool.wait_ge(sent[k], 32 * (NT // RING))

        sems.clear()


def experts(nc, dram, const):
    LOOPS = (TILES - 2) // 2
    with ExitStack() as ctx:
        def sb(name, shape, dt=F32):
            return ctx.enter_context(nc.sbuf_tensor(f"p8_{name}", shape, dt))

        banks = Banks(const)

        sems = Sems(nc, ctx, "p8")
        w13, w2 = const["w13"], const["w2"]
        x = [sb(f"x{s}", [P, D]) for s in range(2)]
        xT = [sb(f"xT{s}", [P, DC, P]) for s in range(2)]
        sg = [sb(f"sg{s}", [P, FF]) for s in range(2)]
        g = [sb(f"g{s}", [P, FF]) for s in range(2)]
        gT = [sb(f"gT{s}", [P, FC, P]) for s in range(2)]
        y = [sb(f"y{s}", [P, D]) for s in range(2)]
        px, pg, pu, pgT = banks.take([P, DC, P]), banks.take([P, FF]), banks.take([P, FF]), banks.take([P, FC, P])
        py = [banks.take([P, D]) for s in range(2)]
        (x_in, x_turned, xT_out, gate_done, up_done, silu_out, g_out, g_turned, gT_out, down_done, y_out, y_stored) = (
            sems.two(n) for n in ("x_in", "x_turned", "xT_out", "gate_done", "up_done", "silu_out", "g_out", "g_turned", "gT_out",
                                  "down_done", "y_out", "y_stored"))

        xs = dram["xs"].rearrange("(j p) d -> j p d", p=P)
        ys = dram["ys"].rearrange("(j p) d -> j p d", p=P)

        def steps(eng, step):
            step(0, 0)
            with eng.Fori(0, LOOPS) as i:
                for u in (1, 2):
                    step(i, u)
            step(0, TILES - 1)

        with nc.Block() as block:
            @block.sync
            def _(sp):
                def load(i, u):
                    sp.dma_start(x[u % 2][:], xs[2 * i + u]).then_inc(x_in[u % 2], 16)

                def store(i, u):
                    sp.wait_ge(y_out[u % 2], i + u // 2 + 1)
                    carry(sp, const)
                    sp.dma_start(ys[2 * i + u], y[u % 2][:]).then_inc(y_stored[u % 2], 16)

                def step(i, u):
                    if u + 2 < TILES and not (u == 2 and False):
                        sp.wait_ge(x_turned[u % 2], i + u // 2 + 1)
                        carry(sp, const)
                        load(i, u + 2)
                    if u > 0:
                        store(i, u - 1)

                load(0, 0)
                load(0, 1)
                step(0, 0)
                with sp.Fori(0, LOOPS - 1) as i:
                    for u in (1, 2):
                        step(i, u)
                for u in (TILES - 3, TILES - 2, TILES - 1):
                    step(0, u)
                store(0, TILES - 1)
                for s in range(2):
                    sp.wait_ge(y_stored[s], 16 * TILES // 2)

            @block.vector
            def _(dve):
                def out(i, u):
                    s, n = u % 2, i + u // 2
                    dve.wait_ge(down_done[s], n + 1)
                    dve.wait_ge(y_stored[s], 16 * n)
                    nc.vector.tensor_copy(y[s][:], py[s][:]).then_inc(y_out[s], 1)

                def step(i, u):
                    s, n = u % 2, i + u // 2
                    dve.wait_ge(up_done[s], n + 1)
                    dve.wait_ge(silu_out[s], n + 1)
                    dve.wait_ge(g_turned[s], n)
                    nc.vector.tensor_tensor(g[s][:], pu[:], sg[s][:], ALU.mult).then_inc(g_out[s], 1)
                    if u > 0:
                        out(i, u - 1)

                steps(dve, step)
                out(0, TILES - 1)

            @block.scalar
            def _(act):
                def gT_copy(i, u):
                    s, n = u % 2, i + u // 2
                    act.wait_ge(g_turned[s], n + 1)
                    act.wait_ge(down_done[s], n)
                    nc.scalar.copy(gT[s][:], pgT[:]).then_inc(gT_out[s], 1)

                def xT_copy(i, u):
                    s, n = u % 2, i + u // 2
                    act.wait_ge(x_turned[s], n + 1)
                    act.wait_ge(up_done[s], n)
                    nc.scalar.copy(xT[s][:], px[:]).then_inc(xT_out[s], 1)

                def step(i, u):
                    s, n = u % 2, i + u // 2
                    if u > 0:
                        gT_copy(i, u - 1)
                    act.wait_ge(gate_done[s], n + 1)
                    act.wait_ge(g_out[s], n)
                    nc.scalar.activation(sg[s][:], pg[:], ACT.Silu).then_inc(silu_out[s], 1)
                    if u < TILES - 1:
                        xT_copy(i, u + 1)

                xT_copy(0, 0)
                steps(act, step)
                gT_copy(0, TILES - 1)

            @block.tensor
            def _(pe):
                def turn_x(i, u):
                    s, n = u % 2, i + u // 2
                    pe.wait_ge(x_in[s], 16 * (n + 1))
                    if u > 0:
                        pe.wait_ge(xT_out[1 - s], i + (u - 1) // 2 + 1)
                    for c in range(DC):
                        mm = nc.tensor.transpose(px[:, c, :], x[s][:, c * P:(c + 1) * P], const["ident"][:])
                    mm.then_inc(x_turned[s], 1)

                def turn_g(i, u):
                    s, n = u % 2, i + u // 2
                    pe.wait_ge(g_out[s], n + 1)
                    if u > 0:
                        pe.wait_ge(gT_out[1 - s], i + (u - 1) // 2 + 1)
                    for f in range(FC):
                        mm = nc.tensor.transpose(pgT[:, f, :], g[s][:, f * P:(f + 1) * P], const["ident"][:])
                    mm.then_inc(g_turned[s], 1)

                def expert_of(i, u):
                    return pe.value_load(const["expert"][0:1, bass.ds(2 * i + u, 1)], min_val=0, max_val=E - 1)

                def up(i, u):
                    s, n = u % 2, i + u // 2
                    e = expert_of(i, u)
                    pe.wait_ge(xT_out[s], n + 1)
                    if u > 0:
                        pe.wait_ge(g_out[1 - s], i + (u - 1) // 2 + 1)
                    for out, half, done in ((pg, 0, gate_done), (pu, 1, up_done)):
                        for c in range(DC):
                            mm = nc.tensor.matmul(out[:], xT[s][:, c, :], w13[:, e, c, half * FF:(half + 1) * FF],
                                                  start=(c == 0), stop=(c == DC - 1))
                        mm.then_inc(done[s], 1)

                def down(i, u):
                    s, n = u % 2, i + u // 2
                    e = expert_of(i, u)
                    pe.wait_ge(gT_out[s], n + 1)
                    pe.wait_ge(y_out[s], n)
                    for f in range(FC):
                        mm = nc.tensor.matmul(py[s][:], gT[s][:, f, :], w2[:, e, f, :], start=(f == 0), stop=(f == FC - 1))
                    mm.then_inc(down_done[s], 1)

                def step(i, u):
                    if u > 0:
                        turn_g(i, u - 1)
                    up(i, u)
                    if u < TILES - 1:
                        turn_x(i, u + 1)
                    if u > 0:
                        down(i, u - 1)

                pe.wait_ge(const["w_experts_in"], 16 * 2 * E)
                turn_x(0, 0)
                steps(pe, step)
                turn_g(0, TILES - 1)
                down(0, TILES - 1)

        sems.clear()


def combine(nc, dram, const):
    RING = 4
    with ExitStack() as ctx:
        def sb(name):
            return [ctx.enter_context(nc.sbuf_tensor(f"p9_{name}{k}", [P, D], F32)) for k in range(RING)]

        sems = Sems(nc, ctx, "p9")

        r, y1, y2, t1, t2 = (sb(n) for n in ("r", "y1", "y2", "t1", "t2"))
        r_in, y_in, half, summed, stored = (sems.some(n, RING) for n in ("r_in", "y_in", "half", "summed", "stored"))
        rt = dram["r"].rearrange("b (t p) d -> (b t) p d", p=P)
        out = dram["out"].rearrange("b (t p) d -> (b t) p d", p=P)
        with nc.Block() as block:
            @block.sync
            def _(sp):
                for t in range(NT + 2):
                    if t < NT:
                        k, n = t % RING, t // RING
                        if n:
                            sp.wait_ge(half[k], n)
                        sp.dma_start(r[k][:], rt[t]).then_inc(r_in[k], 16)
                    if t >= 2:
                        k, n = (t - 2) % RING, (t - 2) // RING
                        sp.wait_ge(summed[k], n + 1)
                        sp.dma_start(out[t - 2], t2[k][:]).then_inc(stored[k], 16)
                for k in range(RING):
                    sp.wait_ge(stored[k], 16 * (NT // RING))

            @block.gpsimd
            def _(pool):
                for t in range(NT):
                    k, n = t % RING, t // RING
                    if n:
                        pool.wait_ge(summed[k], n)
                    for e, y in enumerate((y1, y2)):
                        nc.gpsimd.indirect_dma_start(
                            y[k][:], None, dram["ys"], bass.IndirectOffsetOnAxis(ap=const["rows"][:, e, t:t + 1], axis=0),
                            bounds_check=TILES * P - 1).then_inc(y_in[k], 16)

            @block.vector
            def _(dve):
                for t in range(NT):
                    k, n = t % RING, t // RING
                    dve.wait_ge(y_in[k], 32 * (n + 1))
                    dve.wait_ge(r_in[k], 16 * (n + 1))
                    nc.vector.scalar_tensor_tensor(t1[k][:], y1[k][:], const["weight"][:, 0, t:t + 1], r[k][:],
                                                   ALU.mult, ALU.add).then_inc(half[k], 1)
                    dve.wait_ge(half[k], n + 1)
                    if n:
                        dve.wait_ge(stored[k], 16 * n)
                    nc.vector.scalar_tensor_tensor(t2[k][:], y2[k][:], const["weight"][:, 1, t:t + 1], t1[k][:],
                                                   ALU.mult, ALU.add).then_inc(summed[k], 1)


def build(nc, dram):
    with ExitStack() as ctx:
        def internal(name, shape):
            dram[name] = nc.dram_tensor(name, shape, F32, kind="Internal").ap()

        for n in ("q1qh", "q1ql", "q1kh", "q1kl", "q2qh", "q2ql"):
            internal(n, [B, D, S])
        for n in ("q1v", "q1o", "q2o", "x1", "z", "r", "h2"):
            internal(n, [B, S, D])
        for n in ("q2kh", "q2kl"):
            internal(n, [B, NKV * HD, S])
        internal("q2v", [B, S, NKV * HD])
        internal("xs", [TILES * P, D])
        internal("ys", [TILES * P, D])

        const = {"carried": ctx.enter_context(nc.semaphore("carried")),
                 "w_experts_in": ctx.enter_context(nc.semaphore("w_experts_in"))}
        shapes = {"ident": [P, P], "ones": [P, P], "before": [P, P], "neg_half": [P, TC], "eps": [P, TC], "inv_d": [P, TC],
                  "iota_e": [P, E], "iota_less": [P, E], "iota_j": [P, TILES], "logits": [P, NT, E], "weight": [P, 2, NT],
                  "mask": [P, P], "zero": [P, D]}
        for n, shape in shapes.items():
            const[n] = ctx.enter_context(nc.sbuf_tensor(n, shape, F32))
        for n, shape in (("ident_r", [P, P]), ("mask_r", [P, 3 * P])):
            const[n] = ctx.enter_context(nc.sbuf_tensor(n, shape, F32R))
        const["psum"] = ctx.enter_context(nc.psum_tensor("psum", [P, 8 * BANK], F32))
        const["rows"] = ctx.enter_context(nc.sbuf_tensor("rows", [P, 2, NT], U32))
        const["expert"] = ctx.enter_context(nc.sbuf_tensor("expert", [1, TILES], I32))

        filled = ctx.enter_context(nc.semaphore("filled"))
        xs_zeroed = ctx.enter_context(nc.semaphore("xs_zeroed"))
        with nc.Block() as block:
            @block.gpsimd
            def _(pool):
                g = nc.gpsimd
                n = 0
                for name, value in (("neg_half", -0.5), ("eps", EPS), ("inv_d", 1.0 / D), ("ident", 0.0), ("ones", 1.0), ("before", 1.0),
                                    ("mask", 0.0), ("zero", 0.0)):
                    g.memset(const[name][:], value).then_inc(filled, 1)
                    n += 1
                pool.wait_ge(filled, n)
                g.affine_select(out=const["ident"][:], in_=const["ident"][:], compare_op=ALU.not_equal, fill=1.0, base=0,
                                pattern=[[-1, P]], channel_multiplier=1).then_inc(filled, 1)
                g.affine_select(out=const["before"][:], in_=const["before"][:], compare_op=ALU.is_gt, fill=0.0, base=0,
                                pattern=[[1, P]], channel_multiplier=-1).then_inc(filled, 1)
                g.affine_select(out=const["mask"][:], in_=const["mask"][:], compare_op=ALU.is_ge, fill=NEG, base=0,
                                pattern=[[-1, P]], channel_multiplier=1).then_inc(filled, 1)
                g.iota(const["iota_e"][:], pattern=[[1, E]], base=0, channel_multiplier=0, allow_small_or_imprecise_dtypes=True).then_inc(filled, 1)
                g.iota(const["iota_less"][:], pattern=[[1, E]], base=-E, channel_multiplier=0, allow_small_or_imprecise_dtypes=True).then_inc(filled, 1)
                g.iota(const["iota_j"][:], pattern=[[1, TILES]], base=0, channel_multiplier=0, allow_small_or_imprecise_dtypes=True).then_inc(filled, 1)

            @block.vector
            def _(dve):
                dve.wait_ge(filled, 14)
                nc.vector.tensor_copy(const["ident_r"][:], const["ident"][:]).then_inc(filled, 1)
                nc.vector.memset(const["mask_r"][:, 0:P].bitcast(F32), 0.0).then_inc(filled, 1)
                for c in (1, 2):
                    nc.vector.tensor_copy(const["mask_r"][:, c * P:(c + 1) * P], const["mask"][:]).then_inc(filled, 1)

            @block.scalar
            def _(act):
                act.wait_ge(filled, 14)
                act.dma_start(dram["xs"].rearrange("(j p) d -> p j d", p=P),
                              const["zero"][:].rearrange("p (j d) -> p j d", j=1).to_broadcast([P, TILES, D])).then_inc(xs_zeroed, 16)

        project_first(nc, dram, const)
        attention(nc, dram, const, "q1", NH, False)
        for n, shape in (("w13", [P, E, DC, 2 * FF]), ("w2", [P, E, FC, D])):
            const[n] = ctx.enter_context(nc.sbuf_tensor(f"experts_{n}", shape, F32))
        middle(nc, dram, const)
        with nc.Block() as block:
            @block.scalar
            def _(act):
                for e in range(E):
                    act.dma_start(const["w13"][:, e], dram["w13"][e].rearrange("(c p) o -> p c o", p=P)).then_inc(const["w_experts_in"], 16)
                    act.dma_start(const["w2"][:, e], dram["w2"][e].rearrange("(c p) o -> p c o", p=P)).then_inc(const["w_experts_in"], 16)
                act.wait_ge(xs_zeroed, 16)
        attention(nc, dram, const, "q2", NKV, True)
        finish_attention(nc, dram, const)
        route(nc, dram, const)
        dispatch(nc, dram, const)
        experts(nc, dram, const)
        combine(nc, dram, const)


def kernel(**inputs):
    import numpy as _np
    import concourse.bacc as _bacc
    from concourse import mybir as _mybir
    from concourse.bass_utils import run_bass_kernel_spmd as _run

    nc = _bacc.Bacc("TRN2", target_bir_lowering=False, num_devices=1)

    def as_is(name):
        return _np.ascontiguousarray(inputs[name])

    def turned(name):
        return _np.ascontiguousarray(_np.swapaxes(_np.asarray(inputs[name]), -1, -2))

    inv_freq = _np.float32(1.0) / _np.float32(10000.0) ** (_np.arange(0, HD, 2, dtype=_np.float32) / _np.float32(HD))
    angle = _np.arange(S, dtype=_np.float32)[:, None] * inv_freq[None, :]
    cos = _np.concatenate([_np.cos(angle), _np.cos(angle)], axis=-1)
    sin = _np.concatenate([-_np.sin(angle), _np.sin(angle)], axis=-1)

    data = {"x": as_is("x"), "ctx": as_is("ctx_1024"),
            "wq1": turned("L0_xattn_Wq"), "bq": as_is("L0_xattn_bq"), "wk1": turned("L0_xattn_Wk"), "bk": as_is("L0_xattn_bk"),
            "wv1": turned("L0_xattn_Wv"), "bv": as_is("L0_xattn_bv"), "wo1": turned("L0_xattn_Wo"), "bo": as_is("L0_xattn_bo"),
            "ln1": as_is("L0_ffn_ln1_w"), "ln2": as_is("L0_ffn_ln2_w"), "wqkv": turned("L0_ffn_wqkv"), "wo2": turned("L0_ffn_wo"),
            "gate": turned("L0_ffn_gate_w"), "w13": turned("L0_ffn_w13"), "w2": turned("L0_ffn_w2"), "cos": cos, "sin": sin}
    arrays = {f"in_{n}": a for n, a in data.items()}
    dram = {n: nc.dram_tensor(f"in_{n}", a.shape, _mybir.dt.from_np(a.dtype), kind="ExternalInput").ap() for n, a in data.items()}
    dram["out"] = nc.dram_tensor("out_0", (B, S, D), F32, kind="ExternalOutput").ap()
    build(nc, dram)
    r = _run(nc, [arrays], core_ids=[0])
    return r.results[0]["out_0"]
```

```python
from contextlib import ExitStack

import concourse.bass as bass
import numpy as np
from concourse import mybir

F32 = mybir.dt.float32
F32R = mybir.dt.float32r
I32 = mybir.dt.int32
U32 = mybir.dt.uint32
ALU = mybir.AluOpType
ACT = mybir.ActivationFunctionType
AX = mybir.AxisListType

P = 128
D = 256
DC = D // P
S = 256
TC = S // P
B = 16
PAIRS = B // 2
NH = 16
HD = D // NH
NKV = 4
HP = NH // 2
EPS = 1e-5
E = 8
FF = 512
FC = FF // P
NT = B * TC
TILES = 2 * NT + E
BANK = 512
NEG = -1.0e30
SCALE = float(HD) ** -0.5


class Sems:

    def __init__(self, nc, ctx, tag):
        self.nc, self.ctx, self.tag, self.taken = nc, ctx, tag, []

    def one(self, name):
        sem = self.ctx.enter_context(self.nc.semaphore(f"{self.tag}_{name}"))
        self.taken.append(sem.num)
        return sem

    def some(self, name, n):
        return [self.one(f"{name}{s}") for s in range(n)]

    def two(self, name):
        return self.some(name, 2)

    def clear(self):
        nums = sorted(self.taken)
        starts = [n for n in nums if n - 1 not in nums]
        ends = [n + 1 for n in nums if n + 1 not in nums]
        with self.nc.Block() as block:
            @block.gpsimd
            def _(pool):
                for start, end in zip(starts, ends):
                    pool.sem_clear(range(start, end))


def carry(eng, const):
    eng.sem_inc(const["carried"], 1)


class Banks:

    def __init__(self, const):
        self.psum, self.used = const["psum"], 0

    def take(self, shape):
        size = int(np.prod(shape[1:]))
        view = self.psum[:, self.used:self.used + size]
        self.used += -(-size // BANK) * BANK
        assert self.used <= 8 * BANK
        if len(shape) == 3:
            view = view.rearrange("p (a b) -> p a b", b=shape[2])
        return view


def project_first(nc, dram, const):
    SLOTS = 4
    TURNS = B // SLOTS
    with ExitStack() as ctx:
        def sb(name, shape, dt=F32):
            return ctx.enter_context(nc.sbuf_tensor(f"p1_{name}", shape, dt))

        sems = Sems(nc, ctx, "p1")
        wq, wk, wv = (sb(n, [P, DC, D]) for n in ("wq", "wk", "wv"))
        bq, bk = sb("bq", [P, DC]), sb("bk", [P, DC])
        bv = sb("bv", [P, D])
        x = [sb(f"x{s}", [P, TC, D]) for s in range(SLOTS)]
        c = [sb(f"c{s}", [P, TC, D]) for s in range(SLOTS)]
        st = [sb(f"st{s}", [P, TC, 6]) for s in range(SLOTS)]
        mv = [sb(f"mv{s}", [P, TC, 2]) for s in range(SLOTS)]
        ve = [sb(f"ve{s}", [P, TC]) for s in range(SLOTS)]
        rs = [sb(f"rs{s}", [P, TC]) for s in range(SLOTS)]
        xn = [sb(f"xn{s}", [P, TC, D]) for s in range(SLOTS)]
        xT = [sb(f"xT{s}", [P, DC, S]) for s in range(SLOTS)]
        cT = [sb(f"cT{s}", [P, DC, S]) for s in range(SLOTS)]
        hi = {n: [sb(f"{n}h{s}", [P, DC, S], F32R) for s in range(SLOTS)] for n in "qk"}
        lo = {n: [sb(f"{n}l{s}", [P, DC, S], F32R) for s in range(SLOTS)] for n in "qk"}
        v = [sb(f"v{s}", [P, TC, NH, HD]) for s in range(SLOTS)]
        banks = Banks(const)
        pT = {n: banks.take([P, DC, S]) for n in "xc"}
        pP = {n: [banks.take([P, 2, 256]) for k in range(2)] for n in "qkv"}

        w_in = sems.one("w_in")
        x_in, c_in = sems.some("x_in", SLOTS), sems.some("c_in", SLOTS)
        stats, moments, eps_added, rstd = (sems.some(n, SLOTS) for n in ("stats", "moments", "eps_added", "rstd"))
        normed = sems.some("normed", SLOTS)
        turned_x, turned_c = sems.some("turned_x", SLOTS), sems.some("turned_c", SLOTS)
        xT_out, cT_out = sems.some("xT_out", SLOTS), sems.some("cT_out", SLOTS)
        proj = {n: sems.some(f"proj_{n}", SLOTS) for n in "qkv"}
        hi_out = {n: sems.some(f"hi_{n}", SLOTS) for n in "qk"}
        lo_out = {n: sems.some(f"lo_{n}", SLOTS) for n in "qk"}
        v_out = sems.some("v_out", SLOTS)
        qk_stored, v_stored = sems.some("qk_stored", SLOTS), sems.some("v_stored", SLOTS)
        W_DMAS = 6 * 16

        with nc.Block() as block:
            @block.sync
            def _(sp):
                def load(i, s):
                    sp.dma_start(x[s][:], dram["x"][SLOTS * i + s].rearrange("(t p) d -> p t d", p=P)).then_inc(x_in[s], 16)
                    sp.dma_start(c[s][:], dram["ctx"][SLOTS * i + s].rearrange("(t p) d -> p t d", p=P)).then_inc(c_in[s], 16)

                def store(i, s):
                    b = SLOTS * i + s
                    for n in "qk":
                        sp.wait_ge(hi_out[n][s], DC * (i + 1))
                        sp.wait_ge(lo_out[n][s], DC * (i + 1))
                        for part, tile in (("h", hi), ("l", lo)):
                            sp.dma_start(dram[f"q1{n}{part}"][b].rearrange("(c p) t -> p c t", p=P),
                                         tile[n][s][:].bitcast(F32)).then_inc(qk_stored[s], 16)
                    sp.wait_ge(v_out[s], i + 1)
                    sp.dma_start(dram["q1v"][b].rearrange("(t p) n -> p t n", p=P),
                                 v[s][:].rearrange("p t h e -> p t (h e)")).then_inc(v_stored[s], 16)

                load(0, 0)
                for w, n in ((wq, "wq1"), (wk, "wk1"), (wv, "wv1")):
                    sp.dma_start(w[:], dram[n].rearrange("(c p) o -> p c o", p=P)).then_inc(w_in, 16)
                with nc.allow_non_contiguous_dma(reason="a column of biases"):
                    sp.dma_start(bq[:], dram["bq"].rearrange("(c p) -> p c", p=P)).then_inc(w_in, 16)
                    sp.dma_start(bk[:], dram["bk"].rearrange("(c p) -> p c", p=P)).then_inc(w_in, 16)
                sp.dma_start(bv[:], dram["bv"].partition_broadcast(P)).then_inc(w_in, 16)
                for s in range(1, SLOTS):
                    load(0, s)
                with sp.Fori(0, TURNS - 1) as i:
                    for s in range(SLOTS):
                        sp.wait_ge(normed[s], TC * (i + 1))
                        sp.wait_ge(turned_c[s], i + 1)
                        load(i + 1, s)
                    for s in range(SLOTS):
                        store(i, s)
                for s in range(SLOTS):
                    store(TURNS - 1, s)
                for s in range(SLOTS):
                    sp.wait_ge(qk_stored[s], 4 * 16 * TURNS)
                    sp.wait_ge(v_stored[s], 16 * TURNS)

            @block.gpsimd
            def _(pool):
                with pool.Fori(0, TURNS) as i:
                    for s in range(SLOTS):
                        pool.wait_ge(moments[s], TC * (i + 1))
                        nc.gpsimd.tensor_tensor(ve[s][:], mv[s][:, :, 1], const["eps"][:, 0:TC], ALU.add).then_inc(eps_added[s], 1)
                        pool.wait_ge(eps_added[s], i + 1)
                        nc.gpsimd.tensor_tensor(rs[s][:], ve[s][:], const["neg_half"][:, 0:TC], ALU.pow).then_inc(rstd[s], 1)

            @block.vector
            def _(dve):
                with dve.Fori(0, TURNS) as i:
                    for s in range(SLOTS):
                        dve.wait_ge(x_in[s], 16 * (i + 1))
                        for t in range(TC):
                            nc.vector.bn_stats(st[s][:, t, :], x[s][:, t, :]).then_inc(stats[s], 1)
                        dve.wait_ge(stats[s], TC * (i + 1))
                        carry(dve, const)
                        for t in range(TC):
                            nc.vector.bn_aggr(mv[s][:, t, :], st[s][:, t, :]).then_inc(moments[s], 1)
                    for s in range(SLOTS):
                        dve.wait_ge(rstd[s], i + 1)
                        dve.wait_ge(turned_x[s], i)
                        for t in range(TC):
                            nc.vector.tensor_scalar(xn[s][:, t, :], x[s][:, t, :], mv[s][:, t, 0:1], rs[s][:, t:t + 1],
                                                    ALU.subtract, ALU.mult).then_inc(normed[s], 1)
                    for s in range(SLOTS):
                        dve.wait_ge(turned_x[s], i + 1)
                        dve.wait_ge(proj["q"][s], i)
                        nc.vector.tensor_copy(xT[s][:], pT["x"][:]).then_inc(xT_out[s], 1)
                    for s in range(SLOTS):
                        dve.wait_ge(qk_stored[s], 4 * 16 * i)
                        for n, bias in (("q", bq), ("k", bk)):
                            dve.wait_ge(hi_out[n][s], DC * (i + 1))
                            for o in range(DC):
                                nc.vector.scalar_tensor_tensor(
                                    lo[n][s][:, o, :], pP[n][s % 2][:, o, :], bias[:, o:o + 1], hi[n][s][:, o, :].bitcast(F32),
                                    ALU.add, ALU.subtract).then_inc(lo_out[n][s], 1)
                        dve.wait_ge(proj["v"][s], i + 1)
                        dve.wait_ge(v_stored[s], 16 * i)
                        nc.vector.tensor_tensor(
                            v[s][:], pP["v"][s % 2][:].rearrange("p t (h e) -> p t h e", h=NH),
                            bv[:].rearrange("p (u h e) -> p u h e", u=1, h=NH).to_broadcast([P, TC, NH, HD]),
                            ALU.add).then_inc(v_out[s], 1)

            @block.scalar
            def _(act):
                act.wait_ge(w_in, W_DMAS)
                with act.Fori(0, TURNS) as i:
                    for s in range(SLOTS):
                        act.wait_ge(turned_c[s], i + 1)
                        act.wait_ge(proj["v"][s], i)
                        nc.scalar.copy(cT[s][:], pT["c"][:]).then_inc(cT_out[s], 1)
                    for s in range(SLOTS):
                        act.wait_ge(qk_stored[s], 4 * 16 * i)
                        for n, bias in (("q", bq), ("k", bk)):
                            act.wait_ge(proj[n][s], i + 1)
                            for o in range(DC):
                                nc.scalar.activation(hi[n][s][:, o, :], pP[n][s % 2][:, o, :], ACT.Identity,
                                                     bias=bias[:, o:o + 1]).then_inc(hi_out[n][s], 1)

            @block.tensor
            def _(pe):
                pe.wait_ge(w_in, W_DMAS)
                with pe.Fori(0, TURNS) as i:
                    for s in range(SLOTS):
                        pe.wait_ge(c_in[s], 16 * (i + 1))
                        pe.wait_ge(cT_out[(s - 1) % SLOTS], i + (s > 0))
                        for cc in range(DC):
                            for t in range(TC):
                                mm = nc.tensor.transpose(pT["c"][:, cc, t * P:(t + 1) * P], c[s][:, t, cc * P:(cc + 1) * P], const["ident"][:])
                        mm.then_inc(turned_c[s], 1)
                        pe.wait_ge(normed[s], TC * (i + 1))
                        pe.wait_ge(xT_out[(s - 1) % SLOTS], i + (s > 0))
                        for cc in range(DC):
                            for t in range(TC):
                                mm = nc.tensor.transpose(pT["x"][:, cc, t * P:(t + 1) * P], xn[s][:, t, cc * P:(cc + 1) * P], const["ident"][:])
                        mm.then_inc(turned_x[s], 1)
                    for s in range(SLOTS):
                        pe.wait_ge(cT_out[s], i + 1)
                        for n, w, src in (("k", wk, cT), ("v", None, cT), ("q", wq, xT)):
                            if n == "q":
                                pe.wait_ge(xT_out[s], i + 1)
                            if n == "v":
                                pe.wait_ge(v_out[(s + 2) % SLOTS], i + s // 2)
                                for t in range(TC):
                                    for cc in range(DC):
                                        mm = nc.tensor.matmul(pP[n][s % 2][:, t, :], src[s][:, cc, t * P:(t + 1) * P], wv[:, cc, :],
                                                              start=(cc == 0), stop=(cc == DC - 1))
                            else:
                                pe.wait_ge(lo_out[n][(s + 2) % SLOTS], DC * (i + s // 2))
                                for o in range(DC):
                                    for cc in range(DC):
                                        mm = nc.tensor.matmul(pP[n][s % 2][:, o, :], w[:, cc, o * P:(o + 1) * P], src[s][:, cc, :],
                                                              start=(cc == 0), stop=(cc == DC - 1))
                            mm.then_inc(proj[n][s], 1)

        sems.clear()


def attention(nc, dram, const, tag, kv_heads, causal):
    SLOTS = 4
    LOOPS = B // SLOTS - 1
    GROUP = NH // kv_heads
    KG = HP if kv_heads == NH else kv_heads
    NB1 = 3 if causal else 2
    W1 = P if causal else S
    W2 = S + P if causal else 2 * S
    VW = 2 * HD
    QUADS = NH // 4
    HQ = NH // 2
    QK_DMAS = 12 * 16
    RELAY_DMAS = 4 * 16

    with ExitStack() as ctx:
        def sb(name, shape, dt=F32):
            return ctx.enter_context(nc.sbuf_tensor(f"{tag}_{name}", shape, dt))

        banks = Banks(const)

        phase_sems = Sems(nc, ctx, tag)
        sems = phase_sems.some

        qs = [sb(f"qs{u}", [P, HP, S], F32R) for u in range(SLOTS)]
        ks = [sb(f"ks{u}", [P, KG, S], F32R) for u in range(SLOTS)]
        vc = [sb(f"vc{u}", [P, TC, kv_heads, HD]) for u in range(SLOTS)]
        v = [sb(f"v{u}", [P, TC, kv_heads, VW]) for u in range(SLOTS)]
        mx = [sb(f"mx{r}", [P, NB1, P]) for r in range(2)]
        nmh = [sb(f"nmh{u}", [NH, S], F32R) for u in range(SLOTS)]
        nml = [sb(f"nml{u}", [NH, S], F32R) for u in range(SLOTS)]
        w = [sb(f"w{g}", [P, 4, W2]) for g in range(QUADS)]
        oT = [sb(f"oT{h}", [P, 2, S]) for h in range(2)]
        rec = [sb(f"rec{h}", [P, TC, HQ]) for h in range(2)]
        o = [sb(f"o{r}", [P, TC, NH, HD]) for r in range(2)]
        ps1 = [banks.take([P, 2 * S]) for r in range(2)]
        ps2 = [banks.take([P, 2, 2 * S]) for r in range(2)]
        pso = [banks.take([P, 2, S]) for h in range(2)]

        k_ones, v_ones = sems("ones", 2)
        qk_in, v_in, v_padded = sems("qk_in", SLOTS), sems("v_in", SLOTS), sems("v_padded", SLOTS)
        s1_ready, s1_used = sems("s1_ready", 2), sems("s1_used", 2)
        max_done = sems("max_done", 1)[0]
        nmh_done, relayed = sems("nmh_done", SLOTS), sems("relayed", SLOTS)
        s2_ready, exp_done = sems("s2_ready", 2), sems("exp_done", 2)
        masked, w_used = sems("masked", QUADS), sems("w_used", QUADS)
        oT_out, rec_done, o_out, o_stored = sems("oT_out", 2), sems("rec_done", 2), sems("o_out", 2), sems("o_stored", 2)

        def col(h):
            return (h % 2) * HP + h // 2

        def kslot(h):
            return h // 2 if kv_heads == NH else h // GROUP

        def items(u):
            found = []
            for p in range(HP):
                if p == 1 and u + 1 < B:
                    found.append((p, "turn", u + 1))
                if u + 2 < B:
                    found += [(p, "score", (u + 2, h)) for h in (2 * p, 2 * p + 1)]
                if p == 2 and u > 0:
                    found.append((p, "sums", (u - 1, 1)))
                if p == 6:
                    found.append((p, "sums", (u, 0)))
            return found

        FIRST = [(0, "score", (0, h)) for h in range(NH)] + [(0, "turn", 0)] + [(0, "score", (1, h)) for h in range(NH)]
        LAST = [(0, "sums", (B - 1, 1))]
        STEP = len(items(1))
        assert SLOTS * STEP % 2 == 0

        def numbered(i, u):
            n = len(FIRST) + sum(len(items(k)) for k in range(u))
            return [(p, what, x, (n + k) % 2, SLOTS * STEP // 2 * i + (n + k) // 2) for k, (p, what, x) in enumerate(items(u))]

        def first_items():
            return [(p, what, x, k % 2, k // 2) for k, (p, what, x) in enumerate(FIRST)]

        def last_items():
            n = len(FIRST) + sum(len(items(k)) for k in range(B))
            return [(0, what, x, (n + k) % 2, (n + k) // 2) for k, (_, what, x) in enumerate(LAST)]

        def steps(eng, step):
            step(0, 0)
            with eng.Fori(0, LOOPS) as i:
                for u in range(1, SLOTS + 1):
                    step(i, u)
            for u in range(SLOTS * LOOPS + 1, B):
                step(0, u)

        with nc.Block() as block:
            @block.sync
            def _(sp):
                def load(i, u):
                    b, k = SLOTS * i + u, u % SLOTS
                    for par in range(2):
                        r0 = 64 * par
                        for row, part in ((0, "h"), (HD, "l"), (2 * HD, "h")):
                            src = dram[f"{tag}q{part}"][b].rearrange("(j e r) t -> e r j t", e=2, r=HD)[par]
                            sp.dma_start(qs[k][r0 + row:r0 + row + HD, :, :].bitcast(F32), src).then_inc(qk_in[k], 16)
                        for row, part in ((0, "h"), (HD, "h"), (2 * HD, "l")):
                            if kv_heads == NH:
                                src = dram[f"{tag}k{part}"][b].rearrange("(j e r) t -> e r j t", e=2, r=HD)[par]
                            else:
                                src = dram[f"{tag}k{part}"][b].rearrange("(j r) t -> r j t", r=HD)
                            sp.dma_start(ks[k][r0 + row:r0 + row + HD, :, :].bitcast(F32), src).then_inc(qk_in[k], 16)
                    sp.dma_start(vc[k][:].rearrange("p t h e -> p t (h e)"),
                                 dram[f"{tag}v"][b].rearrange("(t p) n -> p t n", p=P)).then_inc(v_in[k], 16)

                def relay(u, q, m):
                    sp.wait_ge(s1_used[q], m + 1)
                    for par in range(2):
                        for k, part in enumerate((nmh, nml)):
                            row = 64 * par + 3 * HD + k
                            sp.dma_start(qs[u % SLOTS][row:row + 1, :, :].bitcast(F32),
                                         part[u % SLOTS][par * HP:(par + 1) * HP, :].bitcast(F32)).then_inc(relayed[u % SLOTS], 16)

                def store(i, u):
                    b = SLOTS * i + u
                    for h in range(2):
                        sp.wait_ge(o_out[h], b + 1)
                    carry(sp, const)
                    sp.dma_start(dram[f"{tag}o"][b].rearrange("(t p) d -> p t d", p=P),
                                 o[u % 2][:].rearrange("p t h e -> p t (h e)")).then_inc(o_stored[u % 2], 16)

                def relays(found):
                    for _, what, x, q, m in found:
                        if what == "turn":
                            relay(x, q, m)

                def step(i, u):
                    if u + 3 < B:
                        sp.wait_ge(w_used[QUADS - 1], SLOTS * i + u)
                        carry(sp, const)
                        load(i, u + 3)
                    relays(numbered(i, u))
                    if u > 0:
                        store(i, u - 1)

                sp.wait_ge(k_ones, 4)
                for u in range(3):
                    load(0, u)
                relays(first_items())
                steps(sp, step)
                store(0, B - 1)
                for r in range(2):
                    sp.wait_ge(o_stored[r], 16 * B // 2)

            @block.gpsimd
            def _(pool):
                for u in range(SLOTS):
                    ins = nc.gpsimd.memset(v[u][:], 1.0)
                ins.then_inc(v_ones, 1)
                pool.wait_ge(v_ones, 1)

                def pad(i, u):
                    k = u % SLOTS
                    pool.wait_ge(v_in[k], 16 * (i + u // SLOTS + 1))
                    carry(pool, const)
                    nc.gpsimd.tensor_copy(v[k][:, :, :, 0:HD], vc[k][:]).then_inc(v_padded[k], 1)

                def step(i, u):
                    if u + 2 < B:
                        pad(i, u + 2)
                    if causal:
                        for p in range(HP):
                            n = HP * u + p
                            pool.wait_ge(exp_done[n % 2], HP * SLOTS // 2 * i + n // 2 + 1)
                            carry(pool, const)
                            for e in range(2):
                                view = w[p // 2][:, 2 * (p % 2) + e, :].rearrange("p (c q) -> p c q", q=P)[:, 0:3:2, :]
                                ins = nc.gpsimd.affine_select(out=view, in_=view, compare_op=ALU.is_ge, fill=0.0, base=0,
                                                              pattern=[[0, 2], [1, P]], channel_multiplier=-1)
                            if p % 2:
                                ins.then_inc(masked[p // 2], 1)

                pad(0, 0)
                pad(0, 1)
                steps(pool, step)

            @block.vector
            def _(dve):
                def maximum(i, u, h, q, m):
                    dve.wait_ge(s1_ready[q], m + 1)
                    nc.vector.tensor_reduce(mx[u % 2][:, :, col(h)], ps1[q][:, 0:NB1 * W1].rearrange("p (c k) -> p c k", k=W1),
                                            AX.X, ALU.max).then_inc(s1_used[q], 1)
                    if causal and h == NH - 1:
                        dve.wait_ge(s1_used[1 - q], m + q)
                        dve.wait_ge(s1_used[q], m + 1)
                        nc.vector.tensor_tensor(mx[u % 2][:, 1, 0:NH], mx[u % 2][:, 1, 0:NH], mx[u % 2][:, 0, 0:NH], ALU.max).then_inc(max_done, 1)

                def negate(i, u, q, m):
                    k, g = u % SLOTS, i + u // SLOTS
                    dve.wait_ge(s1_ready[q], m + 1)
                    dve.wait_ge(relayed[k], RELAY_DMAS * g)
                    nc.vector.tensor_scalar(nmh[k][:], ps1[q][0:NH, 0:S], -1.0, None, ALU.mult).then_inc(nmh_done[k], 1)
                    dve.wait_ge(nmh_done[k], g + 1)
                    nc.vector.scalar_tensor_tensor(nml[k][:], ps1[q][0:NH, 0:S], -1.0, nmh[k][:].bitcast(F32),
                                                   ALU.mult, ALU.subtract).then_inc(s1_used[q], 1)

                def normalise(i, u, h, q, m):
                    b = SLOTS * i + u
                    sums = ps1[q][:].rearrange("p (t h e) -> p t h e", t=TC, e=VW)
                    dve.wait_ge(s1_ready[q], m + 1)
                    nc.vector.reciprocal(rec[h][:], sums[:, :, :, HD]).then_inc(rec_done[h], 1)
                    dve.wait_ge(rec_done[h], b + 1)
                    dve.wait_ge(o_stored[u % 2], 16 * ((SLOTS // 2) * i + u // 2))
                    nc.vector.tensor_tensor(o[u % 2][:, :, h * HQ:(h + 1) * HQ, :], sums[:, :, :, 0:HD],
                                            rec[h][:].rearrange("p t (h e) -> p t h e", e=1).to_broadcast([P, TC, HQ, HD]),
                                            ALU.mult).then_inc(o_out[h], 1)
                    dve.wait_ge(o_out[h], b + 1)
                    dve.sem_inc(s1_used[q], 1)

                def handle(i, found):
                    for _, what, x, q, m in found:
                        if what == "score":
                            maximum(i, *x, q, m)
                        elif what == "turn":
                            negate(i, x, q, m)
                        else:
                            normalise(i, *x, q, m)

                for u in range(SLOTS):
                    for par in range(2):
                        r0 = 64 * par + 2 * HD
                        nc.vector.memset(ks[u][r0:r0 + HD + 2, :, :].bitcast(F32), 1.0)
                for r in range(2):
                    nc.vector.memset(mx[r][:], 0.0).then_inc(k_ones, 1)
                    nc.vector.memset(ps2[r][:], 0.0).then_inc(k_ones, 1)
                dve.wait_ge(k_ones, 4)
                handle(0, first_items())
                steps(dve, lambda i, u: handle(i, numbered(i, u)))
                handle(0, last_items())

            @block.scalar
            def _(act):
                def exponentials(i, u, p):
                    n, g = HP * u + p, p // 2
                    q = n % 2
                    act.wait_ge(s2_ready[q], HP * SLOTS // 2 * i + n // 2 + 1)
                    act.wait_ge(w_used[g], SLOTS * i + u)
                    nc.scalar.activation(w[g][:, 2 * (p % 2):2 * (p % 2) + 2, :], ps2[q][:, :, 0:W2], ACT.Exp,
                                         scale=SCALE).then_inc(exp_done[q], 1)

                def sums_out(i, u, h):
                    b = SLOTS * i + u
                    act.wait_ge(w_used[2 * h + 1], b + 1)
                    act.wait_ge(o_out[h], b)
                    nc.scalar.copy(oT[h][:], pso[h][:]).then_inc(oT_out[h], 1)

                def step(i, u):
                    for p in range(HP):
                        exponentials(i, u, p)
                        if p == 0 and u > 0:
                            sums_out(i, u - 1, 1)
                        if p == 5:
                            sums_out(i, u, 0)

                steps(act, step)
                sums_out(0, B - 1, 1)

            @block.tensor
            def _(pe):
                def scores_for_max(u, h, q):
                    k = u % SLOTS
                    r0, j = 64 * (h % 2), h // 2
                    qa = qs[k][r0:r0 + 3 * HD, j, :]
                    ka = ks[k][r0:r0 + 3 * HD, kslot(h), :]
                    out = ps1[q]
                    if causal:
                        nc.tensor.matmul(out[:, 0:3 * P], const["ident_r"][:], const["mask_r"][:], start=True, stop=False)
                        nc.tensor.matmul(out[:, 0:S], qa[:, P:S], ka, start=False, stop=False)
                        return nc.tensor.matmul(out[:, S:3 * P], qa[:, 0:P], ka[:, 0:P], start=False, stop=True)
                    for t in range(TC):
                        mm = nc.tensor.matmul(out[:, t * S:(t + 1) * S], qa[:, t * P:(t + 1) * P], ka, start=True, stop=True)
                    return mm

                def scores(i, u, h):
                    n = HP * u + h // 2
                    q, k = n % 2, u % SLOTS
                    r0, j = 64 * (h % 2), h // 2
                    if h == 0:
                        pe.wait_ge(relayed[k], RELAY_DMAS * (i + u // SLOTS + 1))
                    if h % 2 == 0:
                        pe.wait_ge(exp_done[q], HP * SLOTS // 2 * i + n // 2)
                    qa = qs[k][r0:r0 + 3 * HD + 2, j, :]
                    ka = ks[k][r0:r0 + 3 * HD + 2, kslot(h), :]
                    out = ps2[q][:, h % 2, :]
                    nc.tensor.matmul(out[:, 0:S], ka[:, 0:P], qa, start=True, stop=True)
                    mm = nc.tensor.matmul(out[:, S:W2], ka[:, P:S], qa[:, P:S] if causal else qa, start=True, stop=True)
                    if h % 2 == 1:
                        mm.then_inc(s2_ready[q], 1)

                def weigh(i, u, g):
                    b, h, k = SLOTS * i + u, g // 2, u % SLOTS
                    for p in (2 * g, 2 * g + 1):
                        n = HP * u + p
                        pe.wait_ge(exp_done[n % 2], HP * SLOTS // 2 * i + n // 2 + 1)
                    if causal:
                        pe.wait_ge(masked[g], b + 1)
                    if g == 0:
                        pe.wait_ge(v_padded[k], i + u // SLOTS + 1)
                    if g % 2 == 0:
                        pe.wait_ge(oT_out[h], b)
                    for c in range(TC):
                        for e in range(4):
                            out = pso[h][32 * e:32 * e + VW, g % 2, :]
                            if causal and c:
                                out = out[:, P:S]
                            mm = nc.tensor.matmul(out, v[k][:, c, (4 * g + e) // GROUP, :],
                                                  w[g][:, e, c * S:W2 if c else S], start=(c == 0), stop=(c == TC - 1))
                    mm.then_inc(w_used[g], 1)

                def handle(i, found, p):
                    for at, what, x, q, m in found:
                        if at != p:
                            continue
                        if what == "score" and x[1] == 0:
                            pe.wait_ge(qk_in[x[0] % SLOTS], QK_DMAS * (i + x[0] // SLOTS + 1))
                        if what == "turn" and causal:
                            pe.wait_ge(max_done, SLOTS * i + x + 1)
                        if what == "turn" and not causal and x in (0, B - 1):
                            pe.wait_ge(s1_used[1 - q], m + q)
                        if what == "sums":
                            pe.wait_ge(oT_out[x[1]], SLOTS * i + x[0] + 1)
                        pe.wait_ge(s1_used[q], m)
                        if what == "score":
                            mm = scores_for_max(*x, q)
                        elif what == "turn":
                            for t in range(TC):
                                mm = nc.tensor.transpose(ps1[q][:, t * P:(t + 1) * P], mx[x % 2][:, 2 if causal and t == 0 else t, :], const["ident"][:])
                        else:
                            for t in range(TC):
                                for g in range(2):
                                    at0 = (2 * t + g) * P
                                    mm = nc.tensor.transpose(ps1[q][:, at0:at0 + P], oT[x[1]][:, g, t * P:(t + 1) * P], const["ident"][:])
                        mm.then_inc(s1_ready[q], 1)
                        yield

                def step(i, u):
                    found = numbered(i, u)
                    for p in range(HP):
                        beside = handle(i, found, p)
                        next(beside, None)
                        scores(i, u, 2 * p)
                        next(beside, None)
                        scores(i, u, 2 * p + 1)
                        for _ in beside:
                            pass
                        if p == 0 and u > 0:
                            weigh(i, u - 1, QUADS - 1)
                        if p in (2, 4, 6):
                            weigh(i, u, p // 2 - 1)

                for _ in handle(0, first_items(), 0):
                    pass
                steps(pe, step)
                weigh(0, B - 1, QUADS - 1)
                for _ in handle(0, last_items(), 0):
                    pass

        phase_sems.clear()


def middle(nc, dram, const):
    QKV = (NH + 2 * NKV) * HD
    ROPED = NH + NKV
    SLOTS = 4
    TURNS = B // SLOTS

    with ExitStack() as ctx:
        def sb(name, shape, dt=F32):
            return ctx.enter_context(nc.sbuf_tensor(f"p3_{name}", shape, dt))

        banks = Banks(const)

        sems = Sems(nc, ctx, "p3")
        wo = sb("wo", [P, DC, D])
        wqkv = sb("wqkv", [P, DC, QKV])
        bo = sb("bo", [P, D])
        ln1 = sb("ln1", [P, D])
        cos, sin = sb("cos", [P, TC, HD]), sb("sin", [P, TC, HD])
        a = [sb(f"a{s}", [P, TC, D]) for s in range(SLOTS)]
        x = [sb(f"x{s}", [P, TC, D]) for s in range(SLOTS)]
        xb = [sb(f"xb{s}", [P, TC, D]) for s in range(SLOTS)]
        aT = [sb(f"aT{s}", [P, DC, S]) for s in range(SLOTS)]
        x1 = [sb(f"x1{s}", [P, TC, D]) for s in range(SLOTS)]
        st = [sb(f"st{s}", [P, TC, 6]) for s in range(SLOTS)]
        mv = [sb(f"mv{s}", [P, TC, 2]) for s in range(SLOTS)]
        sc = [sb(f"sc{s}", [P, 6, TC]) for s in range(SLOTS)]
        z = [sb(f"z{s}", [P, TC, D]) for s in range(SLOTS)]
        h = [sb(f"h{s}", [P, TC, D]) for s in range(SLOTS)]
        hT = [sb(f"hT{s}", [P, DC, S]) for s in range(SLOTS)]
        qc = [sb(f"qc{s}", [P, TC, ROPED, HD]) for s in range(SLOTS)]
        qr = [sb(f"qr{s}", [P, TC, ROPED, HD]) for s in range(SLOTS)]
        qkv = [sb(f"qkv{s}", [P, TC, QKV]) for s in range(SLOTS)]
        qh, ql = ([sb(f"{n}{s}", [P, DC, S], F32R) for s in range(SLOTS)] for n in ("qh", "ql"))
        kh, kl = ([sb(f"{n}{s}", [NKV * HD, S], F32R) for s in range(SLOTS)] for n in ("kh", "kl"))
        low = [banks.take([P, DC, S]) for k in range(4)]
        pa, po, ph = low[0:2], low[2:4], low[0:2]
        pq, pk = (low[2], low[0]), (low[3][:, 0, :], low[1][:, 0, :])
        pp = [[banks.take([P, 2 * S])[:, 0:QKV] for t in range(TC)] for k in range(2)]

        w_in = sems.one("w_in")
        (a_in, x_in, biased, a_turned, aT_out, wo_done, x1_out, stats, moments, scaled, z_out, h_out, h_turned, hT_out,
         qkv_done, v_out, roped_c, roped, qk_turned, qh_out, kh_out, ql_out, kl_out, stored, x1z_stored) = (
            sems.some(n, SLOTS) for n in ("a_in", "x_in", "biased", "a_turned", "aT_out", "wo_done", "x1_out", "stats", "moments",
                                  "scaled", "z_out", "h_out", "h_turned", "hT_out", "qkv_done", "v_out", "roped_c", "roped",
                                  "qk_turned", "qh_out", "kh_out", "ql_out", "kl_out", "stored", "x1z_stored"))
        W_DMAS = 6 * 16

        with nc.Block() as block:
            @block.sync
            def _(sp):
                def load(i, s):
                    b = SLOTS * i + s
                    sp.dma_start(a[s][:], dram["q1o"][b].rearrange("(t p) d -> p t d", p=P)).then_inc(a_in[s], 16)
                    sp.dma_start(x[s][:], dram["x"][b].rearrange("(t p) d -> p t d", p=P)).then_inc(x_in[s], 16)

                def store(i, s):
                    b = SLOTS * i + s
                    for n, tile, ready in (("x1", x1, x1_out), ("z", z, z_out)):
                        sp.wait_ge(ready[s], i + 1)
                        carry(sp, const)
                        sp.dma_start(dram[n][b].rearrange("(t p) d -> p t d", p=P), tile[s][:]).then_inc(x1z_stored[s], 16)
                    for n, tile, ready in (("q2qh", qh, qh_out), ("q2ql", ql, ql_out)):
                        sp.wait_ge(ready[s], i + 1)
                        sp.dma_start(dram[n][b].rearrange("(c p) t -> p c t", p=P), tile[s][:].bitcast(F32)).then_inc(stored[s], 16)
                    for n, tile, ready in (("q2kh", kh, kh_out), ("q2kl", kl, kl_out)):
                        sp.wait_ge(ready[s], i + 1)
                        carry(sp, const)
                        sp.dma_start(dram[n][b], tile[s][:].bitcast(F32)).then_inc(stored[s], 16)
                    sp.dma_start(dram["q2v"][b].rearrange("(t p) n -> p t n", p=P),
                                 qkv[s][:, :, ROPED * HD:QKV]).then_inc(stored[s], 16)

                load(0, 0)
                for tile, n in ((wo, "wo1"), (wqkv, "wqkv")):
                    sp.dma_start(tile[:], dram[n].rearrange("(c p) o -> p c o", p=P)).then_inc(w_in, 16)
                for tile, n in ((cos, "cos"), (sin, "sin")):
                    sp.dma_start(tile[:], dram[n].rearrange("(t p) e -> p t e", p=P)).then_inc(w_in, 16)
                for tile, n in ((bo, "bo"), (ln1, "ln1")):
                    sp.dma_start(tile[:], dram[n].partition_broadcast(P)).then_inc(w_in, 16)
                for s in range(1, SLOTS):
                    load(0, s)
                with sp.Fori(0, TURNS - 1) as i:
                    for s in range(SLOTS):
                        sp.wait_ge(a_turned[s], i + 1)
                        sp.wait_ge(biased[s], i + 1)
                        carry(sp, const)
                        load(i + 1, s)
                    for s in range(SLOTS):
                        store(i, s)
                for s in range(SLOTS):
                    store(TURNS - 1, s)
                for s in range(SLOTS):
                    sp.wait_ge(x1z_stored[s], 2 * 16 * TURNS)
                    sp.wait_ge(stored[s], 5 * 16 * TURNS)

            @block.gpsimd
            def _(pool):
                pool.wait_ge(w_in, W_DMAS)
                with pool.Fori(0, TURNS) as i:
                    for s in range(SLOTS):
                        pool.wait_ge(x_in[s], 16 * (i + 1))
                        pool.wait_ge(x1_out[s], i)
                        nc.gpsimd.tensor_tensor(xb[s][:], x[s][:], bo[:].rearrange("p (t d) -> p t d", t=1).to_broadcast([P, TC, D]),
                                                ALU.add).then_inc(biased[s], 1)
                    for s in range(SLOTS):
                        var = mv[s][:, :, 1]
                        eps, half = const["eps"][:, 0:TC], const["neg_half"][:, 0:TC]
                        pool.wait_ge(moments[s], TC * (i + 1))
                        chain = [(sc[s][:, 0, :], var, eps, ALU.add), (sc[s][:, 1, :], sc[s][:, 0, :], half, ALU.pow),
                                 (sc[s][:, 2, :], var, sc[s][:, 1, :], ALU.mult), (sc[s][:, 3, :], sc[s][:, 2, :], sc[s][:, 1, :], ALU.mult),
                                 (sc[s][:, 4, :], sc[s][:, 3, :], eps, ALU.add), (sc[s][:, 5, :], sc[s][:, 4, :], half, ALU.pow)]
                        for k, (out, in0, in1, op) in enumerate(chain):
                            if k:
                                pool.wait_ge(scaled[s], len(chain) * i + k)
                            nc.gpsimd.tensor_tensor(out, in0, in1, op).then_inc(scaled[s], 1)
                    for s in range(SLOTS):
                        pool.wait_ge(roped_c[s], 3 * TC * (i + 1))
                        pool.wait_ge(stored[s], 5 * 16 * i)
                        nc.gpsimd.tensor_tensor(qkv[s][:, :, 0:ROPED * HD].rearrange("p t (h e) -> p t h e", e=HD), qc[s][:], qr[s][:],
                                                ALU.add).then_inc(roped[s], 1)

            @block.vector
            def _(dve):
                dve.wait_ge(w_in, W_DMAS)
                with dve.Fori(0, TURNS) as i:
                    for s in range(SLOTS):
                        dve.wait_ge(wo_done[s], i + 1)
                        dve.wait_ge(biased[s], i + 1)
                        dve.wait_ge(x1z_stored[s], 2 * 16 * i)
                        nc.vector.tensor_tensor(x1[s][:], po[s % 2][:], xb[s][:], ALU.add).then_inc(x1_out[s], 1)
                        dve.wait_ge(x1_out[s], i + 1)
                        for t in range(TC):
                            nc.vector.bn_stats(st[s][:, t, :], x1[s][:, t, :]).then_inc(stats[s], 1)
                        dve.wait_ge(stats[s], TC * (i + 1))
                        carry(dve, const)
                        for t in range(TC):
                            nc.vector.bn_aggr(mv[s][:, t, :], st[s][:, t, :]).then_inc(moments[s], 1)
                    for s in range(SLOTS):
                        dve.wait_ge(scaled[s], 6 * (i + 1))
                        for t in range(TC):
                            ins = nc.vector.tensor_scalar(z[s][:, t, :], x1[s][:, t, :], mv[s][:, t, 0:1], sc[s][:, 1, t:t + 1],
                                                          ALU.subtract, ALU.mult)
                        ins.then_inc(z_out[s], 1)
                        dve.wait_ge(z_out[s], i + 1)
                        dve.wait_ge(h_turned[s], i)
                        for t in range(TC):
                            ins = nc.vector.scalar_tensor_tensor(h[s][:, t, :], z[s][:, t, :], sc[s][:, 5, t:t + 1], ln1[:],
                                                                 ALU.mult, ALU.mult)
                        ins.then_inc(h_out[s], 1)
                    for s in range(SLOTS):
                        dve.wait_ge(qkv_done[s], i + 1)
                        dve.wait_ge(roped[s], i)
                        for t in range(TC):
                            heads = pp[s % 2][t][:, 0:ROPED * HD].rearrange("p (h e) -> p h e", e=HD)

                            def table(tile, e0, e1):
                                return tile[:, t:t + 1, e0:e1].to_broadcast([P, ROPED, e1 - e0])

                            nc.vector.tensor_tensor(qc[s][:, t, :, :], heads, table(cos, 0, HD), ALU.mult).then_inc(roped_c[s], 1)
                            H2 = HD // 2
                            nc.vector.tensor_tensor(qr[s][:, t, :, 0:H2], heads[:, :, H2:HD], table(sin, 0, H2), ALU.mult).then_inc(roped_c[s], 1)
                            nc.vector.tensor_tensor(qr[s][:, t, :, H2:HD], heads[:, :, 0:H2], table(sin, H2, HD), ALU.mult).then_inc(roped_c[s], 1)
                    for s in range(SLOTS):
                        dve.wait_ge(qh_out[s], i + 1)
                        dve.wait_ge(stored[s], 5 * 16 * i)
                        nc.vector.tensor_tensor(ql[s][:], pq[s % 2][:], qh[s][:].bitcast(F32), ALU.subtract).then_inc(ql_out[s], 1)
                        dve.wait_ge(kh_out[s], i + 1)
                        nc.vector.tensor_tensor(kl[s][:], pk[s % 2][0:NKV * HD, :], kh[s][:].bitcast(F32), ALU.subtract).then_inc(kl_out[s], 1)

            @block.scalar
            def _(act):
                with act.Fori(0, TURNS) as i:
                    for s in range(SLOTS):
                        act.wait_ge(a_turned[s], i + 1)
                        act.wait_ge(wo_done[s], i)
                        nc.scalar.copy(aT[s][:], pa[s % 2][:]).then_inc(aT_out[s], 1)
                    for s in range(SLOTS):
                        act.wait_ge(h_turned[s], i + 1)
                        act.wait_ge(qkv_done[s], i)
                        nc.scalar.copy(hT[s][:], ph[s % 2][:]).then_inc(hT_out[s], 1)
                    for s in range(SLOTS):
                        act.wait_ge(qkv_done[s], i + 1)
                        act.wait_ge(roped_c[s], 3 * TC * (i + 1))
                        act.wait_ge(stored[s], 5 * 16 * i)
                        for t in range(TC):
                            nc.scalar.copy(qkv[s][:, t, ROPED * HD:QKV], pp[s % 2][t][:, ROPED * HD:QKV]).then_inc(v_out[s], 1)
                    for s in range(SLOTS):
                        act.wait_ge(qk_turned[s], i + 1)
                        act.wait_ge(stored[s], 5 * 16 * i)
                        nc.scalar.copy(qh[s][:], pq[s % 2][:]).then_inc(qh_out[s], 1)
                        nc.scalar.copy(kh[s][:], pk[s % 2][0:NKV * HD, :]).then_inc(kh_out[s], 1)

            @block.tensor
            def _(pe):
                pe.wait_ge(w_in, W_DMAS)

                def turn(out, src):
                    for c in range(DC):
                        for t in range(TC):
                            mm = nc.tensor.transpose(out[:, c, t * P:(t + 1) * P], src[:, t, c * P:(c + 1) * P], const["ident"][:])
                    return mm

                with pe.Fori(0, TURNS) as i:
                    for s in range(SLOTS):
                        pe.wait_ge(a_in[s], 16 * (i + 1))
                        if s >= 2:
                            pe.wait_ge(aT_out[s - 2], i + 1)
                        else:
                            pe.wait_ge(ql_out[SLOTS - 1], i)
                            pe.wait_ge(kl_out[SLOTS - 1], i)
                        turn(pa[s % 2], a[s]).then_inc(a_turned[s], 1)
                    for s in range(SLOTS):
                        pe.wait_ge(aT_out[s], i + 1)
                        if s >= 2:
                            pe.wait_ge(x1_out[s - 2], i + 1)
                        else:
                            pe.wait_ge(ql_out[SLOTS - 2], i)
                            pe.wait_ge(kl_out[SLOTS - 2], i)
                        for t in range(TC):
                            for c in range(DC):
                                mm = nc.tensor.matmul(po[s % 2][:, t, :], aT[s][:, c, t * P:(t + 1) * P], wo[:, c, :],
                                                      start=(c == 0), stop=(c == DC - 1))
                        mm.then_inc(wo_done[s], 1)
                    for s in range(SLOTS):
                        pe.wait_ge(h_out[s], i + 1)
                        if s >= 2:
                            pe.wait_ge(hT_out[s - 2], i + 1)
                        else:
                            pe.wait_ge(aT_out[s + 2], i + 1)
                        turn(ph[s % 2], h[s]).then_inc(h_turned[s], 1)
                    for s in range(SLOTS):
                        pe.wait_ge(hT_out[s], i + 1)
                        pe.wait_ge(v_out[(s + 2) % SLOTS], TC * (i + s // 2))
                        for t in range(TC):
                            for c in range(DC):
                                mm = nc.tensor.matmul(pp[s % 2][t][:], hT[s][:, c, t * P:(t + 1) * P], wqkv[:, c, :],
                                                      start=(c == 0), stop=(c == DC - 1))
                        mm.then_inc(qkv_done[s], 1)
                    for s in range(SLOTS):
                        pe.wait_ge(roped[s], i + 1)
                        pe.wait_ge(v_out[s], TC * (i + 1))
                        if s >= 2:
                            pe.wait_ge(ql_out[s - 2], i + 1)
                            pe.wait_ge(kl_out[s - 2], i + 1)
                        else:
                            for k in (2, 3):
                                pe.wait_ge((x1_out, hT_out)[s][k], i + 1)
                        for t in range(TC):
                            for c in range(DC + 1):
                                out = pq[s % 2][:, c, t * P:(t + 1) * P] if c < DC else pk[s % 2][:, t * P:(t + 1) * P]
                                mm = nc.tensor.transpose(out, qkv[s][:, t, c * P:(c + 1) * P], const["ident"][:])
                        mm.then_inc(qk_turned[s], 1)

        sems.clear()


def finish_attention(nc, dram, const):
    SLOTS = 4
    TURNS = B // SLOTS
    with ExitStack() as ctx:
        def sb(name, shape, dt=F32):
            return ctx.enter_context(nc.sbuf_tensor(f"p5_{name}", shape, dt))

        banks = Banks(const)

        sems = Sems(nc, ctx, "p5")
        wo = sb("wo", [P, DC, D])
        gate = sb("gate", [P, DC, E])
        ln2 = sb("ln2", [P, D])
        a = [sb(f"a{s}", [P, TC, D]) for s in range(SLOTS)]
        x1 = [sb(f"x1{s}", [P, TC, D]) for s in range(SLOTS)]
        z = [sb(f"z{s}", [P, TC, D]) for s in range(SLOTS)]
        aT = [sb(f"aT{s}", [P, DC, S]) for s in range(SLOTS)]
        z2 = [sb(f"z2{s}", [P, TC, D]) for s in range(SLOTS)]
        r = [sb(f"r{s}", [P, TC, D]) for s in range(SLOTS)]
        sq = [sb(f"sq{s}", [P, TC, D]) for s in range(SLOTS)]
        ms = [sb(f"ms{s}", [P, TC]) for s in range(SLOTS)]
        sc = [sb(f"sc{s}", [P, 3, TC]) for s in range(SLOTS)]
        h = [sb(f"h{s}", [P, TC, D]) for s in range(SLOTS)]
        hT = [sb(f"hT{s}", [P, DC, S]) for s in range(SLOTS)]
        pa = [banks.take([P, DC, S]) for k in range(2)]
        po = [banks.take([P, TC, D]) for k in range(2)]
        ph = [banks.take([P, DC, S]) for k in range(2)]
        pl = [banks.take([P, TC, E]) for k in range(2)]

        w_in = sems.one("w_in")
        (a_in, xz_in, a_turned, aT_out, wo_done, z2_out, r_out, squared, scaled, h_out, h_turned, hT_out, logits_done,
         logits_out, r_stored, h_stored) = (
            sems.some(n, SLOTS) for n in ("a_in", "xz_in", "a_turned", "aT_out", "wo_done", "z2_out", "r_out", "squared", "scaled",
                                  "h_out", "h_turned", "hT_out", "logits_done", "logits_out", "r_stored", "h_stored"))
        W_DMAS = 3 * 16

        with nc.Block() as block:
            @block.sync
            def _(sp):
                def load(i, s):
                    b = SLOTS * i + s
                    sp.dma_start(a[s][:], dram["q2o"][b].rearrange("(t p) d -> p t d", p=P)).then_inc(a_in[s], 16)
                    sp.dma_start(z[s][:], dram["z"][b].rearrange("(t p) d -> p t d", p=P)).then_inc(xz_in[s], 16)
                    sp.dma_start(x1[s][:], dram["x1"][b].rearrange("(t p) d -> p t d", p=P)).then_inc(xz_in[s], 16)

                def store(i, s):
                    b = SLOTS * i + s
                    for n, tile, ready, done in (("r", r, r_out, r_stored), ("h2", h, h_out, h_stored)):
                        sp.wait_ge(ready[s], i + 1)
                        carry(sp, const)
                        sp.dma_start(dram[n][b].rearrange("(t p) d -> p t d", p=P), tile[s][:]).then_inc(done[s], 16)

                load(0, 0)
                sp.dma_start(wo[:], dram["wo2"].rearrange("(c p) o -> p c o", p=P)).then_inc(w_in, 16)
                sp.dma_start(gate[:], dram["gate"].rearrange("(c p) e -> p c e", p=P)).then_inc(w_in, 16)
                sp.dma_start(ln2[:], dram["ln2"].partition_broadcast(P)).then_inc(w_in, 16)
                for s in range(1, SLOTS):
                    load(0, s)
                with sp.Fori(0, TURNS - 1) as i:
                    for s in range(SLOTS):
                        sp.wait_ge(a_turned[s], i + 1)
                        sp.wait_ge(r_out[s], i + 1)
                        carry(sp, const)
                        load(i + 1, s)
                    for s in range(SLOTS):
                        store(i, s)
                for s in range(SLOTS):
                    store(TURNS - 1, s)
                for s in range(SLOTS):
                    sp.wait_ge(r_stored[s], 16 * TURNS)
                    sp.wait_ge(h_stored[s], 16 * TURNS)

            @block.gpsimd
            def _(pool):
                with pool.Fori(0, TURNS) as i:
                    for s in range(SLOTS):
                        pool.wait_ge(xz_in[s], 2 * 16 * (i + 1))
                        pool.wait_ge(z2_out[s], i + 1)
                        pool.wait_ge(r_stored[s], 16 * i)
                        nc.gpsimd.tensor_tensor(r[s][:], x1[s][:], z2[s][:], ALU.add).then_inc(r_out[s], 1)
                    for s in range(SLOTS):
                        pool.wait_ge(squared[s], TC * (i + 1))
                        chain = [(sc[s][:, 0, :], ms[s][:], const["inv_d"][:, 0:TC], ALU.mult),
                                 (sc[s][:, 1, :], sc[s][:, 0, :], const["eps"][:, 0:TC], ALU.add),
                                 (sc[s][:, 2, :], sc[s][:, 1, :], const["neg_half"][:, 0:TC], ALU.pow)]
                        for k, (out, in0, in1, op) in enumerate(chain):
                            if k:
                                pool.wait_ge(scaled[s], len(chain) * i + k)
                            nc.gpsimd.tensor_tensor(out, in0, in1, op).then_inc(scaled[s], 1)

            @block.vector
            def _(dve):
                dve.wait_ge(w_in, W_DMAS)
                with dve.Fori(0, TURNS) as i:
                    for s in range(SLOTS):
                        dve.wait_ge(wo_done[s], i + 1)
                        dve.wait_ge(xz_in[s], 2 * 16 * (i + 1))
                        dve.wait_ge(r_out[s], i)
                        nc.vector.tensor_tensor(z2[s][:], po[s % 2][:], z[s][:], ALU.add).then_inc(z2_out[s], 1)
                    for s in range(SLOTS):
                        dve.wait_ge(scaled[s], 3 * (i + 1))
                        dve.wait_ge(h_stored[s], 16 * i)
                        for t in range(TC):
                            ins = nc.vector.scalar_tensor_tensor(h[s][:, t, :], z2[s][:, t, :], sc[s][:, 2, t:t + 1], ln2[:],
                                                                 ALU.mult, ALU.mult)
                        ins.then_inc(h_out[s], 1)
                    for s in range(SLOTS):
                        dve.wait_ge(logits_done[s], i + 1)
                        nc.vector.tensor_copy(const["logits"][:, bass.ds(SLOTS * TC * i + TC * s, TC), :], pl[s % 2][:]).then_inc(logits_out[s], 1)

            @block.scalar
            def _(act):
                with act.Fori(0, TURNS) as i:
                    for s in range(SLOTS):
                        act.wait_ge(a_turned[s], i + 1)
                        act.wait_ge(wo_done[s], i)
                        nc.scalar.copy(aT[s][:], pa[s % 2][:]).then_inc(aT_out[s], 1)
                    for s in range(SLOTS):
                        act.wait_ge(z2_out[s], i + 1)
                        act.wait_ge(scaled[s], 3 * i)
                        for t in range(TC):
                            nc.scalar.activation(sq[s][:, t, :], z2[s][:, t, :], ACT.Square, accum_out=ms[s][:, t:t + 1]).then_inc(squared[s], 1)
                    for s in range(SLOTS):
                        act.wait_ge(h_turned[s], i + 1)
                        act.wait_ge(logits_done[s], i)
                        nc.scalar.copy(hT[s][:], ph[s % 2][:]).then_inc(hT_out[s], 1)

            @block.tensor
            def _(pe):
                pe.wait_ge(w_in, W_DMAS)

                def turn(out, src):
                    for c in range(DC):
                        for t in range(TC):
                            mm = nc.tensor.transpose(out[:, c, t * P:(t + 1) * P], src[:, t, c * P:(c + 1) * P], const["ident"][:])
                    return mm

                with pe.Fori(0, TURNS) as i:
                    for s in range(SLOTS):
                        pe.wait_ge(a_in[s], 16 * (i + 1))
                        pe.wait_ge(aT_out[(s + 2) % SLOTS], i + s // 2)
                        turn(pa[s % 2], a[s]).then_inc(a_turned[s], 1)
                    for s in range(SLOTS):
                        pe.wait_ge(aT_out[s], i + 1)
                        pe.wait_ge(z2_out[(s + 2) % SLOTS], i + s // 2)
                        for t in range(TC):
                            for c in range(DC):
                                mm = nc.tensor.matmul(po[s % 2][:, t, :], aT[s][:, c, t * P:(t + 1) * P], wo[:, c, :],
                                                      start=(c == 0), stop=(c == DC - 1))
                        mm.then_inc(wo_done[s], 1)
                    for s in range(SLOTS):
                        pe.wait_ge(h_out[s], i + 1)
                        pe.wait_ge(hT_out[(s + 2) % SLOTS], i + s // 2)
                        turn(ph[s % 2], h[s]).then_inc(h_turned[s], 1)
                    for s in range(SLOTS):
                        pe.wait_ge(hT_out[s], i + 1)
                        pe.wait_ge(logits_out[(s + 2) % SLOTS], i + s // 2)
                        for t in range(TC):
                            for c in range(DC):
                                mm = nc.tensor.matmul(pl[s % 2][:, t, :], hT[s][:, c, t * P:(t + 1) * P], gate[:, c, :],
                                                      start=(c == 0), stop=(c == DC - 1))
                        mm.then_inc(logits_done[s], 1)

        sems.clear()


def route(nc, dram, const):
    with ExitStack() as ctx:
        def sb(name, shape, dt=F32):
            return ctx.enter_context(nc.sbuf_tensor(f"p6_{name}", shape, dt))

        big = [P, NT, E]
        lm, eq, idx, tmp, m1, m2, m, cnt, tot, incl, pos = (sb(n, big) for n in ("lm", "eq", "idx", "tmp", "m1", "m2", "m", "cnt", "tot",
                                                                                 "incl", "pos"))
        top, first, diff, ex, den = (sb(n, [P, NT]) for n in ("top", "first", "diff", "ex", "den"))
        top2 = sb("top2", [P, NT])
        ones_t = sb("ones_t", [P, NT])
        nti = sb("nti", [P, E], I32)
        ntf, cum, base = (sb(n, [P, E]) for n in ("ntf", "cum", "base"))
        le = sb("le", [P, TILES, E])
        ef = sb("ef", [P, TILES])
        banks = Banks(const)
        pc, pt = banks.take(big), banks.take(big)
        sems = Sems(nc, ctx, "p6")
        done = sems.one("done")
        counted = sems.one("counted")
        masks = sems.one("masks")
        exped = sems.one("exped")
        diffed = sems.one("diffed")

        def over_experts(tile):
            return tile[:].rearrange("p (t e) -> p t e", e=1).to_broadcast(big)

        def over_tiles(tile, n=NT):
            return tile[:].rearrange("p (t e) -> p t e", t=1).to_broadcast([P, n, E])

        with nc.Block() as block:
            @block.vector
            def _(dve):
                chain = [0]

                def link(ins):
                    chain[0] += 1
                    ins.then_inc(done, 1)
                    dve.wait_ge(done, chain[0])

                tt, v = nc.vector.tensor_tensor, nc.vector
                logits = const["logits"]

                def pick(values, best, mask):
                    link(v.tensor_reduce(best[:], values[:], AX.X, ALU.max))
                    link(tt(eq[:], values[:], over_experts(best), ALU.is_equal))
                    link(tt(idx[:], eq[:], over_tiles(const["iota_less"]), ALU.mult))
                    link(v.tensor_scalar(idx[:], idx[:], float(E), None, ALU.add))
                    link(v.tensor_reduce(first[:], idx[:], AX.X, ALU.min))
                    link(tt(mask[:], over_tiles(const["iota_e"]), over_experts(first), ALU.is_equal))

                link(v.memset(ones_t[:], 1.0))
                pick(logits, top, m1)
                link(v.tensor_scalar(tmp[:], m1[:], -3.0e38, None, ALU.mult))
                link(v.tensor_scalar(lm[:], m1[:], -1.0, 1.0, ALU.mult, ALU.add))
                link(tt(lm[:], lm[:], logits[:], ALU.mult))
                link(tt(lm[:], lm[:], tmp[:], ALU.add))
                pick(lm, top2, m2)
                link(tt(m[:], m1[:], m2[:], ALU.add))
                dve.sem_inc(masks, 1)
                link(tt(diff[:], top2[:], top[:], ALU.subtract))
                dve.sem_inc(diffed, 1)
                dve.wait_ge(counted, 1)
                link(v.tensor_copy(tot[:], pt[:]))
                for e in range(E):
                    link(v.tensor_tensor_scan(incl[:, :, e], ones_t[:], tot[:, :, e], 0.0, ALU.mult, ALU.add))
                link(v.tensor_scalar(nti[:], incl[:, NT - 1, :], float(P - 1), None, ALU.add))
                link(v.tensor_scalar(nti[:], nti[:], P.bit_length() - 1, None, ALU.arith_shift_right))
                link(v.tensor_copy(ntf[:], nti[:]))
                link(v.tensor_tensor_scan(cum[:], ones_t[:, 0:E], ntf[:], 0.0, ALU.mult, ALU.add))
                link(tt(base[:], cum[:], ntf[:], ALU.subtract))
                link(v.tensor_scalar(base[:], base[:], float(P), None, ALU.mult))
                link(tt(pos[:], incl[:], tot[:], ALU.subtract))
                link(tt(pos[:], pos[:], over_tiles(base), ALU.add))
                link(tt(pos[:], pos[:], pc[:], ALU.add))
                for k, mask in enumerate((m1, m2)):
                    link(tt(tmp[:], pos[:], mask[:], ALU.mult))
                    link(v.tensor_reduce(first[:], tmp[:], AX.X, ALU.add))
                    link(v.tensor_copy(const["rows"][:, k, :], first[:]))
                link(tt(le[:], over_tiles(cum, TILES), const["iota_j"][:].rearrange("p (t e) -> p t e", e=1).to_broadcast([P, TILES, E]),
                        ALU.is_le))
                link(v.tensor_reduce(ef[:], le[:], AX.X, ALU.add))
                link(v.tensor_scalar(ef[:], ef[:], float(E - 1), None, ALU.min))
                link(v.tensor_copy(const["expert"][:], ef[0:1, :]))
                dve.wait_ge(exped, 1)
                link(v.tensor_scalar(den[:], ex[:], 1.0, None, ALU.add))
                link(v.reciprocal(const["weight"][:, 0, :], den[:]))
                link(tt(const["weight"][:, 1, :], ex[:], const["weight"][:, 0, :], ALU.mult))

            @block.scalar
            def _(act):
                act.wait_ge(diffed, 1)
                nc.scalar.activation(ex[:], diff[:], ACT.Exp).then_inc(exped, 1)

            @block.tensor
            def _(pe):
                pe.wait_ge(masks, 1)
                flat = m[:].rearrange("p t e -> p (t e)")
                nc.tensor.matmul(pc[:].rearrange("p t e -> p (t e)"), const["before"][:], flat, start=True, stop=True)
                nc.tensor.matmul(pt[:].rearrange("p t e -> p (t e)"), const["ones"][:], flat, start=True, stop=True).then_inc(counted, 1)

        sems.clear()


def dispatch(nc, dram, const):
    RING = 4
    with ExitStack() as ctx:
        h = [ctx.enter_context(nc.sbuf_tensor(f"p7_h{k}", [P, D], F32)) for k in range(RING)]
        sems = Sems(nc, ctx, "p7")
        h_in, sent = (sems.some(n, RING) for n in ("h_in", "sent"))
        h2 = dram["h2"].rearrange("b (t p) d -> (b t) p d", p=P)
        with nc.Block() as block:
            @block.sync
            def _(sp):
                for t in range(NT):
                    if t >= RING:
                        sp.wait_ge(sent[t % RING], 32 * (t // RING))
                    sp.dma_start(h[t % RING][:], h2[t]).then_inc(h_in[t % RING], 16)

            @block.gpsimd
            def _(pool):
                for t in range(NT):
                    pool.wait_ge(h_in[t % RING], 16 * (t // RING + 1))
                    for k in range(2):
                        nc.gpsimd.indirect_dma_start(
                            dram["xs"], bass.IndirectOffsetOnAxis(ap=const["rows"][:, k, t:t + 1], axis=0), h[t % RING][:], None,
                            bounds_check=TILES * P - 1).then_inc(sent[t % RING], 16)
                for k in range(RING):
                    pool.wait_ge(sent[k], 32 * (NT // RING))

        sems.clear()


def experts(nc, dram, const):
    LOOPS = (TILES - 2) // 2
    with ExitStack() as ctx:
        def sb(name, shape, dt=F32):
            return ctx.enter_context(nc.sbuf_tensor(f"p8_{name}", shape, dt))

        banks = Banks(const)

        sems = Sems(nc, ctx, "p8")
        w13, w2 = const["w13"], const["w2"]
        x = [sb(f"x{s}", [P, D]) for s in range(2)]
        xT = [sb(f"xT{s}", [P, DC, P]) for s in range(2)]
        sg = [sb(f"sg{s}", [P, FF]) for s in range(2)]
        g = [sb(f"g{s}", [P, FF]) for s in range(2)]
        gT = [sb(f"gT{s}", [P, FC, P]) for s in range(2)]
        y = [sb(f"y{s}", [P, D]) for s in range(2)]
        px, pg, pu, pgT = banks.take([P, DC, P]), banks.take([P, FF]), banks.take([P, FF]), banks.take([P, FC, P])
        py = [banks.take([P, D]) for s in range(2)]
        (x_in, x_turned, xT_out, gate_done, up_done, silu_out, g_out, g_turned, gT_out, down_done, y_out, y_stored) = (
            sems.two(n) for n in ("x_in", "x_turned", "xT_out", "gate_done", "up_done", "silu_out", "g_out", "g_turned", "gT_out",
                                  "down_done", "y_out", "y_stored"))

        xs = dram["xs"].rearrange("(j p) d -> j p d", p=P)
        ys = dram["ys"].rearrange("(j p) d -> j p d", p=P)

        def steps(eng, step):
            step(0, 0)
            with eng.Fori(0, LOOPS) as i:
                for u in (1, 2):
                    step(i, u)
            step(0, TILES - 1)

        with nc.Block() as block:
            @block.sync
            def _(sp):
                def load(i, u):
                    sp.dma_start(x[u % 2][:], xs[2 * i + u]).then_inc(x_in[u % 2], 16)

                def store(i, u):
                    sp.wait_ge(y_out[u % 2], i + u // 2 + 1)
                    carry(sp, const)
                    sp.dma_start(ys[2 * i + u], y[u % 2][:]).then_inc(y_stored[u % 2], 16)

                def step(i, u):
                    if u + 2 < TILES and not (u == 2 and False):
                        sp.wait_ge(x_turned[u % 2], i + u // 2 + 1)
                        carry(sp, const)
                        load(i, u + 2)
                    if u > 0:
                        store(i, u - 1)

                load(0, 0)
                load(0, 1)
                step(0, 0)
                with sp.Fori(0, LOOPS - 1) as i:
                    for u in (1, 2):
                        step(i, u)
                for u in (TILES - 3, TILES - 2, TILES - 1):
                    step(0, u)
                store(0, TILES - 1)
                for s in range(2):
                    sp.wait_ge(y_stored[s], 16 * TILES // 2)

            @block.vector
            def _(dve):
                def out(i, u):
                    s, n = u % 2, i + u // 2
                    dve.wait_ge(down_done[s], n + 1)
                    dve.wait_ge(y_stored[s], 16 * n)
                    nc.vector.tensor_copy(y[s][:], py[s][:]).then_inc(y_out[s], 1)

                def step(i, u):
                    s, n = u % 2, i + u // 2
                    dve.wait_ge(up_done[s], n + 1)
                    dve.wait_ge(silu_out[s], n + 1)
                    dve.wait_ge(g_turned[s], n)
                    nc.vector.tensor_tensor(g[s][:], pu[:], sg[s][:], ALU.mult).then_inc(g_out[s], 1)
                    if u > 0:
                        out(i, u - 1)

                steps(dve, step)
                out(0, TILES - 1)

            @block.scalar
            def _(act):
                def gT_copy(i, u):
                    s, n = u % 2, i + u // 2
                    act.wait_ge(g_turned[s], n + 1)
                    act.wait_ge(down_done[s], n)
                    nc.scalar.copy(gT[s][:], pgT[:]).then_inc(gT_out[s], 1)

                def xT_copy(i, u):
                    s, n = u % 2, i + u // 2
                    act.wait_ge(x_turned[s], n + 1)
                    act.wait_ge(up_done[s], n)
                    nc.scalar.copy(xT[s][:], px[:]).then_inc(xT_out[s], 1)

                def step(i, u):
                    s, n = u % 2, i + u // 2
                    if u > 0:
                        gT_copy(i, u - 1)
                    act.wait_ge(gate_done[s], n + 1)
                    act.wait_ge(g_out[s], n)
                    nc.scalar.activation(sg[s][:], pg[:], ACT.Silu).then_inc(silu_out[s], 1)
                    if u < TILES - 1:
                        xT_copy(i, u + 1)

                xT_copy(0, 0)
                steps(act, step)
                gT_copy(0, TILES - 1)

            @block.tensor
            def _(pe):
                def turn_x(i, u):
                    s, n = u % 2, i + u // 2
                    pe.wait_ge(x_in[s], 16 * (n + 1))
                    if u > 0:
                        pe.wait_ge(xT_out[1 - s], i + (u - 1) // 2 + 1)
                    for c in range(DC):
                        mm = nc.tensor.transpose(px[:, c, :], x[s][:, c * P:(c + 1) * P], const["ident"][:])
                    mm.then_inc(x_turned[s], 1)

                def turn_g(i, u):
                    s, n = u % 2, i + u // 2
                    pe.wait_ge(g_out[s], n + 1)
                    if u > 0:
                        pe.wait_ge(gT_out[1 - s], i + (u - 1) // 2 + 1)
                    for f in range(FC):
                        mm = nc.tensor.transpose(pgT[:, f, :], g[s][:, f * P:(f + 1) * P], const["ident"][:])
                    mm.then_inc(g_turned[s], 1)

                def expert_of(i, u):
                    return pe.value_load(const["expert"][0:1, bass.ds(2 * i + u, 1)], min_val=0, max_val=E - 1)

                def up(i, u):
                    s, n = u % 2, i + u // 2
                    e = expert_of(i, u)
                    pe.wait_ge(xT_out[s], n + 1)
                    if u > 0:
                        pe.wait_ge(g_out[1 - s], i + (u - 1) // 2 + 1)
                    for out, half, done in ((pg, 0, gate_done), (pu, 1, up_done)):
                        for c in range(DC):
                            mm = nc.tensor.matmul(out[:], xT[s][:, c, :], w13[:, e, c, half * FF:(half + 1) * FF],
                                                  start=(c == 0), stop=(c == DC - 1))
                        mm.then_inc(done[s], 1)

                def down(i, u):
                    s, n = u % 2, i + u // 2
                    e = expert_of(i, u)
                    pe.wait_ge(gT_out[s], n + 1)
                    pe.wait_ge(y_out[s], n)
                    for f in range(FC):
                        mm = nc.tensor.matmul(py[s][:], gT[s][:, f, :], w2[:, e, f, :], start=(f == 0), stop=(f == FC - 1))
                    mm.then_inc(down_done[s], 1)

                def step(i, u):
                    if u > 0:
                        turn_g(i, u - 1)
                    up(i, u)
                    if u < TILES - 1:
                        turn_x(i, u + 1)
                    if u > 0:
                        down(i, u - 1)

                pe.wait_ge(const["w_experts_in"], 16 * 2 * E)
                turn_x(0, 0)
                steps(pe, step)
                turn_g(0, TILES - 1)
                down(0, TILES - 1)

        sems.clear()


def combine(nc, dram, const):
    RING = 4
    with ExitStack() as ctx:
        def sb(name):
            return [ctx.enter_context(nc.sbuf_tensor(f"p9_{name}{k}", [P, D], F32)) for k in range(RING)]

        sems = Sems(nc, ctx, "p9")

        r, y1, y2, t1, t2 = (sb(n) for n in ("r", "y1", "y2", "t1", "t2"))
        r_in, y_in, half, summed, stored = (sems.some(n, RING) for n in ("r_in", "y_in", "half", "summed", "stored"))
        rt = dram["r"].rearrange("b (t p) d -> (b t) p d", p=P)
        out = dram["out"].rearrange("b (t p) d -> (b t) p d", p=P)
        with nc.Block() as block:
            @block.sync
            def _(sp):
                for t in range(NT + 2):
                    if t < NT:
                        k, n = t % RING, t // RING
                        if n:
                            sp.wait_ge(half[k], n)
                        sp.dma_start(r[k][:], rt[t]).then_inc(r_in[k], 16)
                    if t >= 2:
                        k, n = (t - 2) % RING, (t - 2) // RING
                        sp.wait_ge(summed[k], n + 1)
                        sp.dma_start(out[t - 2], t2[k][:]).then_inc(stored[k], 16)
                for k in range(RING):
                    sp.wait_ge(stored[k], 16 * (NT // RING))

            @block.gpsimd
            def _(pool):
                for t in range(NT):
                    k, n = t % RING, t // RING
                    if n:
                        pool.wait_ge(summed[k], n)
                    for e, y in enumerate((y1, y2)):
                        nc.gpsimd.indirect_dma_start(
                            y[k][:], None, dram["ys"], bass.IndirectOffsetOnAxis(ap=const["rows"][:, e, t:t + 1], axis=0),
                            bounds_check=TILES * P - 1).then_inc(y_in[k], 16)

            @block.vector
            def _(dve):
                for t in range(NT):
                    k, n = t % RING, t // RING
                    dve.wait_ge(y_in[k], 32 * (n + 1))
                    dve.wait_ge(r_in[k], 16 * (n + 1))
                    nc.vector.scalar_tensor_tensor(t1[k][:], y1[k][:], const["weight"][:, 0, t:t + 1], r[k][:],
                                                   ALU.mult, ALU.add).then_inc(half[k], 1)
                    dve.wait_ge(half[k], n + 1)
                    if n:
                        dve.wait_ge(stored[k], 16 * n)
                    nc.vector.scalar_tensor_tensor(t2[k][:], y2[k][:], const["weight"][:, 1, t:t + 1], t1[k][:],
                                                   ALU.mult, ALU.add).then_inc(summed[k], 1)


def build(nc, dram):
    with ExitStack() as ctx:
        def internal(name, shape):
            dram[name] = nc.dram_tensor(name, shape, F32, kind="Internal").ap()

        for n in ("q1qh", "q1ql", "q1kh", "q1kl", "q2qh", "q2ql"):
            internal(n, [B, D, S])
        for n in ("q1v", "q1o", "q2o", "x1", "z", "r", "h2"):
            internal(n, [B, S, D])
        for n in ("q2kh", "q2kl"):
            internal(n, [B, NKV * HD, S])
        internal("q2v", [B, S, NKV * HD])
        internal("xs", [TILES * P, D])
        internal("ys", [TILES * P, D])

        const = {"carried": ctx.enter_context(nc.semaphore("carried")),
                 "w_experts_in": ctx.enter_context(nc.semaphore("w_experts_in"))}
        shapes = {"ident": [P, P], "ones": [P, P], "before": [P, P], "neg_half": [P, TC], "eps": [P, TC], "inv_d": [P, TC],
                  "iota_e": [P, E], "iota_less": [P, E], "iota_j": [P, TILES], "logits": [P, NT, E], "weight": [P, 2, NT],
                  "mask": [P, P], "zero": [P, D]}
        for n, shape in shapes.items():
            const[n] = ctx.enter_context(nc.sbuf_tensor(n, shape, F32))
        for n, shape in (("ident_r", [P, P]), ("mask_r", [P, 3 * P])):
            const[n] = ctx.enter_context(nc.sbuf_tensor(n, shape, F32R))
        const["psum"] = ctx.enter_context(nc.psum_tensor("psum", [P, 8 * BANK], F32))
        const["rows"] = ctx.enter_context(nc.sbuf_tensor("rows", [P, 2, NT], U32))
        const["expert"] = ctx.enter_context(nc.sbuf_tensor("expert", [1, TILES], I32))

        filled = ctx.enter_context(nc.semaphore("filled"))
        xs_zeroed = ctx.enter_context(nc.semaphore("xs_zeroed"))
        with nc.Block() as block:
            @block.gpsimd
            def _(pool):
                g = nc.gpsimd
                n = 0
                for name, value in (("neg_half", -0.5), ("eps", EPS), ("inv_d", 1.0 / D), ("ident", 0.0), ("ones", 1.0), ("before", 1.0),
                                    ("mask", 0.0), ("zero", 0.0)):
                    g.memset(const[name][:], value).then_inc(filled, 1)
                    n += 1
                pool.wait_ge(filled, n)
                g.affine_select(out=const["ident"][:], in_=const["ident"][:], compare_op=ALU.not_equal, fill=1.0, base=0,
                                pattern=[[-1, P]], channel_multiplier=1).then_inc(filled, 1)
                g.affine_select(out=const["before"][:], in_=const["before"][:], compare_op=ALU.is_gt, fill=0.0, base=0,
                                pattern=[[1, P]], channel_multiplier=-1).then_inc(filled, 1)
                g.affine_select(out=const["mask"][:], in_=const["mask"][:], compare_op=ALU.is_ge, fill=NEG, base=0,
                                pattern=[[-1, P]], channel_multiplier=1).then_inc(filled, 1)
                g.iota(const["iota_e"][:], pattern=[[1, E]], base=0, channel_multiplier=0, allow_small_or_imprecise_dtypes=True).then_inc(filled, 1)
                g.iota(const["iota_less"][:], pattern=[[1, E]], base=-E, channel_multiplier=0, allow_small_or_imprecise_dtypes=True).then_inc(filled, 1)
                g.iota(const["iota_j"][:], pattern=[[1, TILES]], base=0, channel_multiplier=0, allow_small_or_imprecise_dtypes=True).then_inc(filled, 1)

            @block.vector
            def _(dve):
                dve.wait_ge(filled, 14)
                nc.vector.tensor_copy(const["ident_r"][:], const["ident"][:]).then_inc(filled, 1)
                nc.vector.memset(const["mask_r"][:, 0:P].bitcast(F32), 0.0).then_inc(filled, 1)
                for c in (1, 2):
                    nc.vector.tensor_copy(const["mask_r"][:, c * P:(c + 1) * P], const["mask"][:]).then_inc(filled, 1)

            @block.scalar
            def _(act):
                act.wait_ge(filled, 14)
                act.dma_start(dram["xs"].rearrange("(j p) d -> p j d", p=P),
                              const["zero"][:].rearrange("p (j d) -> p j d", j=1).to_broadcast([P, TILES, D])).then_inc(xs_zeroed, 16)

        project_first(nc, dram, const)
        attention(nc, dram, const, "q1", NH, False)
        middle(nc, dram, const)
        for n, shape in (("w13", [P, E, DC, 2 * FF]), ("w2", [P, E, FC, D])):
            const[n] = ctx.enter_context(nc.sbuf_tensor(f"experts_{n}", shape, F32))
        with nc.Block() as block:
            @block.scalar
            def _(act):
                for e in range(E):
                    act.dma_start(const["w13"][:, e], dram["w13"][e].rearrange("(c p) o -> p c o", p=P)).then_inc(const["w_experts_in"], 16)
                    act.dma_start(const["w2"][:, e], dram["w2"][e].rearrange("(c p) o -> p c o", p=P)).then_inc(const["w_experts_in"], 16)
                act.wait_ge(xs_zeroed, 16)
        attention(nc, dram, const, "q2", NKV, True)
        finish_attention(nc, dram, const)
        route(nc, dram, const)
        dispatch(nc, dram, const)
        experts(nc, dram, const)
        combine(nc, dram, const)


def kernel(**inputs):
    import numpy as _np
    import concourse.bacc as _bacc
    from concourse import mybir as _mybir
    from concourse.bass_utils import run_bass_kernel_spmd as _run

    nc = _bacc.Bacc("TRN2", target_bir_lowering=False, num_devices=1)

    def as_is(name):
        return _np.ascontiguousarray(inputs[name])

    def turned(name):
        return _np.ascontiguousarray(_np.swapaxes(_np.asarray(inputs[name]), -1, -2))

    inv_freq = _np.float32(1.0) / _np.float32(10000.0) ** (_np.arange(0, HD, 2, dtype=_np.float32) / _np.float32(HD))
    angle = _np.arange(S, dtype=_np.float32)[:, None] * inv_freq[None, :]
    cos = _np.concatenate([_np.cos(angle), _np.cos(angle)], axis=-1)
    sin = _np.concatenate([-_np.sin(angle), _np.sin(angle)], axis=-1)

    data = {"x": as_is("x"), "ctx": as_is("ctx_1024"),
            "wq1": turned("L0_xattn_Wq"), "bq": as_is("L0_xattn_bq"), "wk1": turned("L0_xattn_Wk"), "bk": as_is("L0_xattn_bk"),
            "wv1": turned("L0_xattn_Wv"), "bv": as_is("L0_xattn_bv"), "wo1": turned("L0_xattn_Wo"), "bo": as_is("L0_xattn_bo"),
            "ln1": as_is("L0_ffn_ln1_w"), "ln2": as_is("L0_ffn_ln2_w"), "wqkv": turned("L0_ffn_wqkv"), "wo2": turned("L0_ffn_wo"),
            "gate": turned("L0_ffn_gate_w"), "w13": turned("L0_ffn_w13"), "w2": turned("L0_ffn_w2"), "cos": cos, "sin": sin}
    arrays = {f"in_{n}": a for n, a in data.items()}
    dram = {n: nc.dram_tensor(f"in_{n}", a.shape, _mybir.dt.from_np(a.dtype), kind="ExternalInput").ap() for n, a in data.items()}
    dram["out"] = nc.dram_tensor("out_0", (B, S, D), F32, kind="ExternalOutput").ap()
    build(nc, dram)
    r = _run(nc, [arrays], core_ids=[0])
    return r.results[0]["out_0"]
```
